# Optimizing a Trainium2 kernel written in Bass

```python
import numpy as np
import jax
import jax.numpy as jnp

def _softmax(x, axis=-1):
    return jax.nn.softmax(x, axis=axis)

def _gelu(x):
    return jax.nn.gelu(x, approximate=True)

def _silu(x):
    return jax.nn.silu(x)

def _sigmoid(x):
    return jax.nn.sigmoid(x)

def _layernorm(x, axis=-1, eps=1e-05):
    m = jnp.mean(x, axis=axis, keepdims=True)
    v = jnp.var(x, axis=axis, keepdims=True)
    return (x - m) / jnp.sqrt(v + eps)

def _scatter_add(tgt, idx, src, axis=0):
    return tgt.at[idx].add(src)

def _segment_sum(src, seg, n):
    return jax.ops.segment_sum(src, seg, n)
kernel_name = 'mk_prb_d2_jaxref_r4_b72f57'

def setup_inputs(seed: int=0):
    np.random.seed(seed)
    _w = jnp.asarray

    def _L0_attn_setup():
        import jax, jax.numpy as jnp
        import numpy as np
        N_Q, N_KV = (16, 4)

        def _rope(x):
            d = x.shape[-1]
            T = x.shape[-2]
            inv_freq = 1.0 / 10000.0 ** (jnp.arange(d // 2, dtype=jnp.float32) * 2.0 / d)
            emb = jnp.arange(T, dtype=jnp.float32)[:, None] * inv_freq[None, :]
            cos, sin = (jnp.cos(emb), jnp.sin(emb))
            x1, x2 = (x[..., 0::2], x[..., 1::2])
            return jnp.concatenate([x1 * cos - x2 * sin, x1 * sin + x2 * cos], axis=-1)
        key = jax.random.key(seed)
        ks = jax.random.split(key, 5)
        B, T, C = (4, 512, 512)
        g = N_Q // N_KV
        Ckv = C // g
        s = 0.02
        return {'x': jax.random.normal(ks[0], (B, T, C), dtype=jnp.float32), 'Wq': jax.random.normal(ks[1], (C, C), dtype=jnp.float32) * s, 'bq': jnp.zeros((C,), dtype=jnp.float32), 'Wk': jax.random.normal(ks[2], (C, Ckv), dtype=jnp.float32) * s, 'bk': jnp.zeros((Ckv,), dtype=jnp.float32), 'Wv': jax.random.normal(ks[3], (C, Ckv), dtype=jnp.float32) * s, 'bv': jnp.zeros((Ckv,), dtype=jnp.float32), 'Wo': jax.random.normal(ks[4], (Ckv, C), dtype=jnp.float32) * s, 'bo': jnp.zeros((C,), dtype=jnp.float32)}
    _L0_attn_in = _L0_attn_setup()

    def _L0_ffn_setup():
        import jax, jax.numpy as jnp
        import numpy as np
        E, TOPK, H, I = (8, 2, 512, 1024)
        SOFTCAP = 30.0
        key = jax.random.key(seed)
        ks = jax.random.split(key, 5)
        s = 1.0 / np.sqrt(H)
        si = 1.0 / np.sqrt(I)
        return {'hidden_states': jax.random.normal(ks[0], (4, 512, H), jnp.float32), 'w_gate': jax.random.normal(ks[1], (H, E), jnp.float32) * s, 'w1': jax.random.normal(ks[2], (E, H, I), jnp.float32) * s, 'w3': jax.random.normal(ks[3], (E, H, I), jnp.float32) * s, 'w2': jax.random.normal(ks[4], (E, I, H), jnp.float32) * si}
    _L0_ffn_in = _L0_ffn_setup()

    def _L1_attn_setup():
        import jax, jax.numpy as jnp
        import numpy as np
        HIDDEN = 512
        HEADS = 16
        HEAD_DIM = HIDDEN // HEADS
        NEG = -10000000000.0
        key = jax.random.key(seed)
        k1, k2, k3 = jax.random.split(key, 3)
        x = jax.random.normal(k1, (2, 512, HIDDEN), dtype=jnp.float32)
        w_qkv = jax.random.normal(k2, (HIDDEN, 3 * HIDDEN), dtype=jnp.float32) / np.sqrt(HIDDEN)
        w_out = jax.random.normal(k3, (HIDDEN, HIDDEN), dtype=jnp.float32) / np.sqrt(HIDDEN)
        return {'x': x, 'w_qkv': w_qkv, 'w_out': w_out}
    _L1_attn_in = _L1_attn_setup()

    def _L1_ffn_setup():
        import jax, jax.numpy as jnp
        import numpy as np
        B, S, D, H = (8, 1024, 512, 1280)

        def ternarize_weight(w):
            abs_mean = jnp.maximum(jnp.mean(jnp.abs(w)), 1e-05)
            thr = 0.7 * abs_mean
            one = jnp.ones((), dtype=w.dtype)
            q = jnp.where(w > thr, one, jnp.where(w < -thr, -one, jnp.zeros((), dtype=w.dtype)))
            return w + jax.lax.stop_gradient(q * abs_mean - w)
        key = jax.random.key(seed)
        k1, k2, k3 = jax.random.split(key, 3)
        x = jax.random.normal(k1, (B, S, D), dtype=jnp.float32)
        w_fc = jax.random.normal(k2, (H, D), dtype=jnp.float32) / np.sqrt(D).astype(np.float32)
        w_proj = jax.random.normal(k3, (D, H), dtype=jnp.float32) / np.sqrt(H).astype(np.float32)
        return {'x': x, 'w_fc': w_fc, 'w_proj': w_proj}
    _L1_ffn_in = _L1_ffn_setup()
    _d = {'L0_attn_x': _L0_attn_in['x'], 'L0_attn_Wq': _L0_attn_in['Wq'], 'L0_attn_bq': _L0_attn_in['bq'], 'L0_attn_Wk': _L0_attn_in['Wk'], 'L0_attn_bk': _L0_attn_in['bk'], 'L0_attn_Wv': _L0_attn_in['Wv'], 'L0_attn_bv': _L0_attn_in['bv'], 'L0_attn_Wo': _L0_attn_in['Wo'], 'L0_attn_bo': _L0_attn_in['bo'], 'L0_ffn_w_gate': _L0_ffn_in['w_gate'], 'L0_ffn_w1': _L0_ffn_in['w1'], 'L0_ffn_w3': _L0_ffn_in['w3'], 'L0_ffn_w2': _L0_ffn_in['w2'], 'L1_attn_w_qkv': _L1_attn_in['w_qkv'], 'L1_attn_w_out': _L1_attn_in['w_out'], 'L1_ffn_w_fc': _L1_ffn_in['w_fc'], 'L1_ffn_w_proj': _L1_ffn_in['w_proj']}
    _x0 = _d['L0_attn_x']
    _d['L0_attn_x'] = jax.random.normal(jax.random.fold_in(jax.random.key(seed), 1), (4, 512, 512), dtype=_x0.dtype)
    del _x0
    return _d

def reference(L0_attn_x, L0_attn_Wq, L0_attn_bq, L0_attn_Wk, L0_attn_bk, L0_attn_Wv, L0_attn_bv, L0_attn_Wo, L0_attn_bo, L0_ffn_w_gate, L0_ffn_w1, L0_ffn_w3, L0_ffn_w2, L1_attn_w_qkv, L1_attn_w_out, L1_ffn_w_fc, L1_ffn_w_proj):

    def _L0_attn_ref(x, Wq, bq, Wk, bk, Wv, bv, Wo, bo):
        import jax, jax.numpy as jnp
        import numpy as np
        N_Q, N_KV = (16, 4)

        def _rope(x):
            d = x.shape[-1]
            T = x.shape[-2]
            inv_freq = 1.0 / 10000.0 ** (jnp.arange(d // 2, dtype=jnp.float32) * 2.0 / d)
            emb = jnp.arange(T, dtype=jnp.float32)[:, None] * inv_freq[None, :]
            cos, sin = (jnp.cos(emb), jnp.sin(emb))
            x1, x2 = (x[..., 0::2], x[..., 1::2])
            return jnp.concatenate([x1 * cos - x2 * sin, x1 * sin + x2 * cos], axis=-1)
        B, T, C = x.shape
        g = N_Q // N_KV
        d = C // N_Q
        q = (x @ Wq + bq).reshape(B, T, N_Q, d).transpose(0, 2, 1, 3)
        k = (x @ Wk + bk).reshape(B, T, N_KV, d).transpose(0, 2, 1, 3)
        v = (x @ Wv + bv).reshape(B, T, N_KV, d).transpose(0, 2, 1, 3)
        q = _rope(q)
        k = _rope(k)
        qg = q.reshape(B, N_KV, g, T, d)
        scores = jnp.einsum('bhgnd,bhsd->bhns', qg, k) * (1.0 / jnp.sqrt(jnp.float32(d)))
        mask = jnp.tril(jnp.ones((T, T), dtype=bool))
        att = jax.nn.softmax(jnp.where(mask, scores, -jnp.inf), axis=-1)
        y = jnp.einsum('bhns,bhsd->bhnd', att, v)
        y = y.transpose(0, 2, 1, 3).reshape(B, T, C // g)
        return y @ Wo + bo

    def _L0_ffn_ref(hidden_states, w_gate, w1, w3, w2):
        import jax, jax.numpy as jnp
        import numpy as np
        E, TOPK, H, I = (8, 2, 512, 1024)
        SOFTCAP = 30.0
        orig_shape = hidden_states.shape
        x = hidden_states.reshape(-1, H)
        logits = x @ w_gate
        logits = SOFTCAP * jnp.tanh(logits / SOFTCAP)
        probs = jax.nn.softmax(logits, axis=-1)
        _, idx = jax.lax.top_k(probs, TOPK)
        mask = jax.nn.one_hot(idx, E, dtype=probs.dtype).sum(-2)
        weights = probs * mask
        out = jnp.zeros_like(x)
        for e in range(E):
            h = jax.nn.silu(x @ w1[e]) * (x @ w3[e])
            out = out + h @ w2[e] * weights[:, e:e + 1]
        return out.reshape(orig_shape)

    def _L1_attn_ref(x, w_qkv, w_out):
        import jax, jax.numpy as jnp
        import numpy as np
        HIDDEN = 512
        HEADS = 16
        HEAD_DIM = HIDDEN // HEADS
        NEG = -10000000000.0
        b, s, _ = x.shape
        qkv = x @ w_qkv
        qkv = qkv.reshape(b, s, 3, HEADS, HEAD_DIM)
        q, k, v = (qkv[:, :, 0], qkv[:, :, 1], qkv[:, :, 2])
        scale = jnp.sqrt(jnp.float32(HEAD_DIM)).astype(x.dtype)
        q = q / scale
        scores = jnp.einsum('bqhd,bkhd->bhqk', q, k)
        causal_mask = jnp.arange(s)[:, None] >= jnp.arange(s)[None, :]
        scores = jnp.where(causal_mask[None, None], scores, NEG)
        attn = jax.nn.softmax(scores, axis=-1)
        out = jnp.einsum('bhqk,bkhd->bqhd', attn, v).reshape(b, s, HIDDEN)
        return out @ w_out

    def _L1_ffn_ref(x, w_fc, w_proj):
        import jax, jax.numpy as jnp
        import numpy as np
        B, S, D, H = (8, 1024, 512, 1280)

        def ternarize_weight(w):
            abs_mean = jnp.maximum(jnp.mean(jnp.abs(w)), 1e-05)
            thr = 0.7 * abs_mean
            one = jnp.ones((), dtype=w.dtype)
            q = jnp.where(w > thr, one, jnp.where(w < -thr, -one, jnp.zeros((), dtype=w.dtype)))
            return w + jax.lax.stop_gradient(q * abs_mean - w)
        h = jnp.einsum('bsd,hd->bsh', x, ternarize_weight(w_fc))
        h = jnp.square(jax.nn.relu(h))
        return jnp.einsum('bsh,dh->bsd', h, ternarize_weight(w_proj))
    x = L0_attn_x
    xn = _layernorm(x, axis=-1)
    x = x + _L0_attn_ref(xn, L0_attn_Wq, L0_attn_bq, L0_attn_Wk, L0_attn_bk, L0_attn_Wv, L0_attn_bv, L0_attn_Wo, L0_attn_bo) + _L0_ffn_ref(xn, L0_ffn_w_gate, L0_ffn_w1, L0_ffn_w3, L0_ffn_w2)
    xn = _layernorm(x, axis=-1)
    x = x + _L1_attn_ref(xn, L1_attn_w_qkv, L1_attn_w_out) + _L1_ffn_ref(xn, L1_ffn_w_fc, L1_ffn_w_proj)
    return x

_drawn_inputs = setup_inputs


def setup_inputs(seed=0):
    import zlib

    import numpy as np

    out = dict(_drawn_inputs(seed))
    spreads = {'L0_attn_bq': (0.0, 0.8),
     'L0_attn_bk': (0.0, 0.8),
     'L0_attn_bv': (0.0, 0.575),
     'L0_attn_bo': (0.0, 0.1)}
    factors = {'L0_attn_Wq': 8.0, 'L0_attn_Wk': 8.0, 'L0_attn_Wv': 6.073, 'L0_attn_Wo': 3.426}
    for name, (base, spread) in spreads.items():
        noise = np.random.default_rng([zlib.crc32(name.encode()), seed]).standard_normal(out[name].shape)
        drawn = base * np.exp(spread * noise) if base else spread * noise
        out[name] = jnp.asarray(drawn.astype(out[name].dtype))
    for name, factor in factors.items():
        out[name] = (out[name] * factor).astype(out[name].dtype)
    return out
```

```python
from contextlib import ExitStack

import concourse.bass as bass
from concourse import mybir

F32 = mybir.dt.float32
F32R = mybir.dt.float32r
BF16 = mybir.dt.bfloat16
I32 = mybir.dt.int32
ACT = mybir.ActivationFunctionType
ALU = mybir.AluOpType
AX = mybir.AxisListType.X

P = 128
BATCH, SEQ, D = 4, 512, 512
TOKENS = BATCH * SEQ
KC = D // P
RT = SEQ // P
NT = TOKENS // P
HD = 32
EXPERTS, TOPK, INNER = 8, 2, 1024
SOFTCAP = 30.0
HID = 1280
HM = HID // P
EPS = 1e-5
NEG = -1e30

SLOTS = 256
TILES = (TOPK * TOKENS + EXPERTS * (SLOTS - 1)) // SLOTS
NSLOT = TILES * SLOTS
SC = NSLOT // P
CH = 4
CW = INNER // CH
CSUB = CW // P
UPW = KC * CW
CHW = 2 * UPW + CSUB * D


def chain(eng, sem, start):
    count = [0]

    def link(ins):
        count[0] += 1
        ins.then_inc(sem, 1)
        eng.wait_ge(sem, start + count[0])
    return link


def repeat(eng, n, body):
    body(0, True)
    with eng.Fori(1, n) as i:
        body(i, False)


def one(ap, i, pattern):
    return ap[bass.ds(i, 1)].rearrange(pattern)


def build(nc, x, wq, bq, wk, bk, wv, bv, wo, bo, w_gate, w1, w3, w2, w_qkv, w_out, w_fc, w_proj, cos, sin, out):
    ctx = ExitStack()

    def dram(name, shape, dt=F32):
        return nc.dram_tensor(name, shape, dt).ap()

    xn_d = dram("xn_d", (TOKENS, D))
    xt0_d = [dram(f"xt0_{s}", (BATCH, P, KC * SEQ)) for s in ("hi", "lo")]
    xt1_d = [dram(f"xt1_{s}", (BATCH, P, KC * SEQ)) for s in ("hi", "lo")]
    r0_d = dram("r0_d", (TOKENS, D))
    r1_d = dram("r1_d", (TOKENS, D))
    slot_tok_d = dram("slot_tok_d", (NSLOT, 1))
    y_d = dram("y_d", (NSLOT, D))

    def sb(stack, name, shape, dt=F32, side="left"):
        return stack.enter_context(nc.sbuf_tensor(name, shape, dt, side=side))

    def ps(stack, name, shape, dt=F32):
        return stack.enter_context(nc.psum_tensor(name, shape, dt))

    def sem(name):
        return ctx.enter_context(nc.semaphore(name))

    stage_done = sem("stage_done")

    passed = sem("passed")

    def settle(eng):
        eng.sem_inc(passed, 1)

    def end(eng):
        eng.drain().then_inc(stage_done, 1)

    def begin(eng, k):
        if k:
            eng.wait_ge(stage_done, 5 * k)

    ident = sb(ctx, "ident", [P, P])
    ident_b = sb(ctx, "ident_b", [P, P], BF16)
    mask_b = sb(ctx, "mask_b", [P, P], BF16)
    before_b = sb(ctx, "before_b", [P, P], BF16)
    ones_b = sb(ctx, "ones_b", [P, P], BF16)
    ones = sb(ctx, "ones", [P, P])
    slot = sb(ctx, "slot", [P, TOPK, NT], I32)
    slot_w = sb(ctx, "slot_w", [P, TOPK, NT])
    tile_expert = sb(ctx, "tile_expert", [P, TILES + 1], I32)
    slot_token = sb(ctx, "slot_token", [P, SC], I32)
    fc_scale = sb(ctx, "fc_scale", [P, 1])
    proj_scale = sb(ctx, "proj_scale", [P, 1])

    ternary = ExitStack()
    fcT = sb(ternary, "fcT", [P, KC, HID], F32R, side="right")
    projT = sb(ternary, "projT", [P, HM, D], F32R, side="right")

    def prepare_stage():
        st = ExitStack()
        fc = sb(st, "fc_raw", [P, HM, D])
        pr = sb(st, "proj_raw", [P, KC, HID])
        fcb = sb(st, "fc_sign", [P, HM, D], BF16)
        prb = sb(st, "proj_sign", [P, KC, HID], BF16)
        low = sb(st, "below", [P, KC, HID])
        sums = sb(st, "abs_sums", [P, 2, HM])
        tot = sb(st, "abs_tot", [P, 2])
        mean = sb(st, "abs_mean", [P, 2])
        thr = sb(st, "thr", [P, 2, 2])
        tot_ps = ps(st, "tot_ps", [P, 2])
        tp_ps = [ps(st, f"tern_ps{i}", [P, KC, P], BF16) for i in range(2)]
        st.close()
        loaded = sem("tern_loaded")
        const_done = sem("const_done")
        abs_done, tot_done, sum_done = sem("abs_done"), sem("abs_tot_done"), sem("abs_sum_done")
        thr_done = sem("thr_done")
        sign_step = sem("sign_step")
        tern_t, tern_copied = sem("tern_transposed"), sem("tern_copied")
        flat = [fc[:].rearrange("p a b -> p (a b)"), pr[:].rearrange("p a b -> p (a b)")]
        flatb = [fcb[:].rearrange("p a b -> p (a b)"), prb[:].rearrange("p a b -> p (a b)")]
        lowf = low[:].rearrange("p a b -> p (a b)")

        def sp(eng):
            eng.dma_start(fc[:], w_fc.rearrange("(n p) d -> p n d", p=P)).then_inc(loaded, 16)
            eng.dma_start(pr[:], w_proj.rearrange("(n p) h -> p n h", p=P)).then_inc(loaded, 16)

        def pool(eng):
            eng.memset(ident[:], 0.0).then_inc(const_done, 1)
            eng.memset(ident_b[:], 0.0).then_inc(const_done, 1)
            eng.memset(mask_b[:], 0.0).then_inc(const_done, 1)
            eng.memset(before_b[:], 0.0).then_inc(const_done, 1)
            eng.memset(ones_b[:], 1.0).then_inc(const_done, 1)
            eng.memset(ones[:], 1.0).then_inc(const_done, 1)
            eng.wait_ge(const_done, 6)
            for t, op, fill in ((ident, ALU.not_equal, 1.0), (ident_b, ALU.not_equal, 1.0),
                                (mask_b, ALU.is_ge, NEG), (before_b, ALU.is_ge, 1.0)):
                eng.affine_select(out=t[:], in_=t[:], compare_op=op, fill=fill, base=0,
                                  pattern=[[-1, P]], channel_multiplier=1).then_inc(const_done, 1)
            eng.wait_ge(thr_done, 3)
            link = chain(eng, sign_step, 0)
            for m in range(2):
                link(eng.tensor_scalar(lowf, flat[m], thr[:, m, 1:2], None, ALU.is_lt))
                link(eng.tensor_scalar(flat[m], flat[m], thr[:, m, 0:1], None, ALU.is_gt))
                link(eng.tensor_tensor(flatb[m], flat[m], lowf, ALU.subtract))

        def act(eng):
            eng.wait_ge(loaded, 32)
            for m in range(2):
                for n in range(HM):
                    part = flat[m][:, n * D:(n + 1) * D]
                    last = nc.scalar.activation(flatb[m][:, n * D:(n + 1) * D], part, ACT.Abs, accum_out=sums[:, m, n:n + 1])
            last.then_inc(abs_done, 1)
            for k in range(HM):
                eng.wait_ge(tern_t, k + 1)
                nc.scalar.copy(fcT[:, :, k * P:(k + 1) * P], tp_ps[k % 2][:]).then_inc(tern_copied, 1)
            for k in range(HM):
                eng.wait_ge(tern_t, HM + k + 1)
                nc.scalar.copy(projT[:, k, :], tp_ps[k % 2][:].rearrange("p a b -> p (a b)")).then_inc(tern_copied, 1)

        def dve(eng):
            eng.wait_ge(abs_done, 1)
            eng.tensor_reduce(tot[:], sums[:], AX, ALU.add).then_inc(tot_done, 1)
            eng.wait_ge(sum_done, 1)
            eng.tensor_scalar(mean[:], tot_ps[:], 1.0 / (HID * D), 1e-5, ALU.mult, ALU.max).then_inc(thr_done, 1)
            eng.wait_ge(thr_done, 1)
            eng.tensor_copy(fc_scale[:], mean[:, 0:1])
            eng.tensor_copy(proj_scale[:], mean[:, 1:2])
            eng.tensor_scalar(thr[:, :, 0], mean[:], 0.7, None, ALU.mult).then_inc(thr_done, 1)
            eng.tensor_scalar(thr[:, :, 1], mean[:], -0.7, None, ALU.mult).then_inc(thr_done, 1)

        def pe(eng):
            eng.wait_ge(const_done, 10)
            eng.wait_ge(tot_done, 1)
            eng.matmul(tot_ps[:], ones[:], tot[:], start=True, stop=True).then_inc(sum_done, 1)
            for k in range(2 * HM):
                m, n = k // HM, k % HM
                eng.wait_ge(sign_step, 3 * m + 3)
                if k >= 2:
                    eng.wait_ge(tern_copied, k - 1)
                for c in range(KC):
                    src = fcb[:, n, c * P:(c + 1) * P] if m == 0 else prb[:, c, n * P:(n + 1) * P]
                    last = eng.transpose(tp_ps[k % 2][:, c, :], src, ident_b[:])
                last.then_inc(tern_t, 1)

        return dict(sp=sp, pool=pool, act=act, dve=dve, pe=pe)

    LN_STEPS = 8

    def norm_buffers(stack, name):
        return dict(stats=sb(stack, name + "_stats", [P, RT, 6]), mv=sb(stack, name + "_mv", [P, RT, 2]),
                    var=sb(stack, name + "_var", [P, RT]), rstd=sb(stack, name + "_rstd", [P, RT]),
                    tmp=sb(stack, name + "_tmp", [P, RT]))

    def layer_norm(dve, src, ln, step, start, sqrt_done, sqrt_value):
        stats, mv, var, rstd, tmp = (ln[n] for n in ("stats", "mv", "var", "rstd", "tmp"))
        link = chain(dve, step, start)
        for t in range(RT):
            last = dve.bn_stats(stats[:, t, :], src[:, t, :])
        link(last)
        settle(dve)
        for t in range(RT):
            last = dve.bn_aggr(mv[:, t, :], stats[:, t, :])
        link(last)
        link(dve.tensor_scalar(var[:], mv[:, :, 1], EPS, None, ALU.add))
        dve.wait_ge(sqrt_done, sqrt_value)
        link(dve.reciprocal(rstd[:], rstd[:]))
        link(dve.tensor_tensor(tmp[:], rstd[:], rstd[:], ALU.mult))
        link(dve.tensor_tensor(tmp[:], tmp[:], var[:], ALU.mult))
        link(dve.tensor_scalar(tmp[:], tmp[:], -0.5, 1.5, ALU.mult, ALU.add))
        link(dve.tensor_tensor(rstd[:], rstd[:], tmp[:], ALU.mult))

    def normed(dve, src, dst, ln):
        for t in range(RT):
            last = dve.tensor_scalar(dst[:, t, :], src[:, t, :], ln["mv"][:, t, 0:1], ln["rstd"][:, t:t + 1],
                                     ALU.subtract, ALU.mult)
        return last

    routing = ExitStack()
    logits = sb(routing, "logits", [P, NT, EXPERTS])

    def norm_stage():
        st = ExitStack()
        xin = sb(st, "xin", [P, RT, D])
        xn = sb(st, "xn", [P, RT, D])
        xth = sb(st, "xt_hi", [P, KC, SEQ], F32R)
        xtl = sb(st, "xt_lo", [P, KC, SEQ], F32R)
        wg = sb(st, "wg", [P, KC, EXPERTS])
        wgh = sb(st, "wg_hi", [P, KC, P], F32R)
        wgl = sb(st, "wg_lo", [P, KC, P], F32R)
        lgT = sb(st, "logitsT", [EXPERTS, SEQ])
        ln = norm_buffers(st, "ln0")
        xt_ps = ps(st, "xt_ps", [P, KC, SEQ])
        lgT_ps = ps(st, "lgT_ps", [P, SEQ])
        lg_ps = ps(st, "lg_ps", [P, RT * EXPERTS])
        st.close()

        x_in = sem("x_in")
        wg_in, wg_zero, wg_split = sem("wg_in"), sem("wg_zero"), sem("wg_split")
        ln_step, sqrt_done = sem("ln0_step"), sem("ln0_sqrt_done")
        xn_ready, xn_stored = sem("xn_ready"), sem("xn_stored")
        xt_done, xth_done, xtl_done = sem("xt_done"), sem("xth_done"), sem("xtl_done")
        xt_stored = sem("xt_stored")
        lgT_done, lgT_copied = sem("lgT_done"), sem("lgT_copied")
        lg_done, lg_copied = sem("lg_done"), sem("lg_copied")

        x_b = x.rearrange("b (t p) d -> b p t d", p=P)
        xn_b = xn_d.rearrange("(b t p) d -> b p t d", b=BATCH, p=P)

        def pool(eng):
            def turn(b, first):
                eng.dma_start(xin[:], one(x_b, b, "a p t d -> (a p) t d")).then_inc(x_in, 16)
                eng.wait_ge(xn_ready, b + 1)
            repeat(eng, BATCH, turn)

        def sp(eng):
            eng.dma_start(wg[:], w_gate.rearrange("(k p) e -> p k e", p=P)).then_inc(wg_in, 16)

            def turn(b, first):
                eng.wait_ge(xn_ready, b + 1)
                eng.dma_start(one(xn_b, b, "a p t d -> (a p) t d"), xn[:]).then_inc(xn_stored, 16)
                eng.wait_ge(xtl_done, KC * b + KC)
                for s, t in enumerate((xth, xtl)):
                    eng.dma_start(one(xt0_d[s], b, "a p n -> (a p) n"),
                                  t[:].bitcast(F32).rearrange("p k n -> p (k n)")).then_inc(xt_stored, 16)
            repeat(eng, BATCH, turn)
            eng.wait_ge(xn_stored, 16 * BATCH)
            eng.wait_ge(xt_stored, 32 * BATCH)

        def act(eng):
            def turn(b, first):
                eng.wait_ge(ln_step, LN_STEPS * b + 3)
                nc.scalar.activation(ln["rstd"][:], ln["var"][:], ACT.Sqrt).then_inc(sqrt_done, 1)
                eng.wait_ge(xt_done, b + 1)
                if not first:
                    eng.wait_ge(xt_stored, 32 * b)
                    eng.wait_ge(lgT_done, b)
                for k in range(KC):
                    nc.scalar.copy(xth[:, k, :], xt_ps[:, k, :]).then_inc(xth_done, 1)
                eng.wait_ge(lgT_done, b + 1)
                nc.scalar.copy(lgT[:], lgT_ps[0:EXPERTS, :]).then_inc(lgT_copied, 1)
                eng.wait_ge(lg_done, b + 1)
                nc.scalar.copy(logits[:].rearrange("p t e -> p (t e)")[:, bass.ds(b * (RT * EXPERTS), RT * EXPERTS)],
                               lg_ps[:]).then_inc(lg_copied, 1)
            repeat(eng, BATCH, turn)

        def dve(eng):
            eng.memset(wgh[:].bitcast(F32), 0.0)
            eng.memset(wgl[:].bitcast(F32), 0.0).then_inc(wg_zero, 1)
            eng.wait_ge(wg_zero, 1)
            eng.wait_ge(wg_in, 16)
            eng.tensor_copy(wgh[:, :, 0:EXPERTS], wg[:]).then_inc(wg_split, 1)
            eng.wait_ge(wg_split, 1)
            eng.tensor_tensor(wgl[:, :, 0:EXPERTS], wg[:], wgh[:, :, 0:EXPERTS].bitcast(F32),
                              ALU.subtract).then_inc(wg_split, 1)

            def turn(b, first):
                eng.wait_ge(x_in, 16 * b + 16)
                layer_norm(eng, xin, ln, ln_step, LN_STEPS * b, sqrt_done, b + 1)
                if not first:
                    eng.wait_ge(xn_stored, 16 * b)
                normed(eng, xin, xn, ln).then_inc(xn_ready, 1)
                if not first:
                    eng.wait_ge(xt_stored, 32 * b)
                    eng.wait_ge(lgT_done, b)
                for k in range(KC):
                    eng.wait_ge(xth_done, KC * b + k + 1)
                    eng.tensor_tensor(xtl[:, k, :], xt_ps[:, k, :], xth[:, k, :].bitcast(F32),
                                      ALU.subtract).then_inc(xtl_done, 1)
            repeat(eng, BATCH, turn)

        def pe(eng):
            eng.wait_ge(wg_split, 2)

            def turn(b, first):
                eng.wait_ge(xn_ready, b + 1)
                if not first:
                    eng.wait_ge(xtl_done, KC * b)
                for k in range(KC):
                    for t in range(RT):
                        last = eng.transpose(xt_ps[:, k, t * P:(t + 1) * P], xn[:, t, k * P:(k + 1) * P], ident[:])
                last.then_inc(xt_done, 1)
                if not first:
                    eng.wait_ge(lgT_copied, b)
                for k in range(KC):
                    eng.wait_ge(xtl_done, KC * b + k + 1)
                    for w, v in ((wgh, xth), (wgh, xtl), (wgl, xth)):
                        last = eng.matmul(lgT_ps[:], w[:, k, :], v[:, k, :], start=(k == 0 and w is wgh and v is xth),
                                          stop=(k == KC - 1 and w is wgl))
                last.then_inc(lgT_done, 1)
                eng.wait_ge(lgT_copied, b + 1)
                if not first:
                    eng.wait_ge(lg_copied, b)
                    settle(eng)
                for t in range(RT):
                    last = eng.transpose(lg_ps[:, t * EXPERTS:(t + 1) * EXPERTS], lgT[:, t * P:(t + 1) * P],
                                         ident[0:EXPERTS, 0:EXPERTS])
                last.then_inc(lg_done, 1)
            repeat(eng, BATCH, turn)

        return dict(sp=sp, pool=pool, act=act, dve=dve, pe=pe)

    def route_stage():
        st = ExitStack()
        shape = [P, NT, EXPERTS]
        probs = sb(st, "probs", shape)
        picked = [sb(st, f"picked{k}", shape) for k in range(TOPK)]
        work = sb(st, "work", shape)
        e_iota = sb(st, "e_iota", shape)
        e_below = sb(st, "e_below", shape)
        row = sb(st, "row", [P, NT])
        chosen = sb(st, "chosen", shape, BF16)
        ahead = sb(st, "ahead", [P, NT + 1, EXPERTS], BF16)
        steps = sb(st, "steps", [P, EXPERTS, EXPERTS])
        tile_i = sb(st, "tile_i", [P, TILES + 1, EXPERTS])
        tile_w = sb(st, "tile_w", [P, TILES + 1, EXPERTS])
        tile_f = sb(st, "tile_f", [P, TILES + 1])
        ntile = sb(st, "ntile", [P, EXPERTS])
        upto = sb(st, "upto", [P, EXPERTS])
        base = sb(st, "base", [P, EXPERTS])
        token = sb(st, "token", [P, NT])
        zero = sb(st, "zero", [SC, P])
        table = sb(st, "table", [SC, P])
        slot_f = sb(st, "slot_f", [P, TOPK, NT])
        rank_ps = ps(st, "rank_ps", [P, NT * EXPERTS])
        count_ps = ps(st, "count_ps", [P, EXPERTS])
        table_ps = ps(st, "table_ps", [P, SC])
        st.close()
        iota_done, zero_done, table_zero = sem("iota_done"), sem("zero_done"), sem("table_zero")
        tanh_ready, tanh_done, exp_ready, exp_done0 = (sem(n) for n in ("tanh_ready", "tanh_done", "exp_ready", "exp_done0"))
        r_step, ahead_done, rank_done = sem("r_step"), sem("ahead_done"), sem("rank_done")
        slot_done, scattered, table_in, table_t, token_done = (
            sem(n) for n in ("slot_done", "scattered", "table_in", "table_t", "token_done"))

        def pool(eng):
            eng.iota(e_iota[:], pattern=[[0, NT], [1, EXPERTS]], base=0, channel_multiplier=0,
                     allow_small_or_imprecise_dtypes=True)
            eng.iota(e_below[:], pattern=[[0, NT], [1, EXPERTS]], base=-EXPERTS, channel_multiplier=0,
                     allow_small_or_imprecise_dtypes=True)
            eng.iota(steps[:], pattern=[[0, EXPERTS], [SLOTS, EXPERTS]], base=0, channel_multiplier=0,
                     allow_small_or_imprecise_dtypes=True)
            eng.iota(tile_i[:], pattern=[[1, TILES + 1], [0, EXPERTS]], base=0, channel_multiplier=0,
                     allow_small_or_imprecise_dtypes=True)
            eng.iota(token[:], pattern=[[P, NT]], base=0, channel_multiplier=1,
                     allow_small_or_imprecise_dtypes=True).then_inc(iota_done, 1)
            eng.memset(zero[:], 0.0).then_inc(zero_done, 1)
            eng.wait_ge(zero_done, 1)
            eng.dma_start(slot_tok_d.rearrange("(c p) o -> c (p o)", p=P), zero[:]).then_inc(table_zero, 16)
            eng.wait_ge(table_zero, 16)
            eng.wait_ge(iota_done, 1)
            eng.wait_ge(slot_done, 1)
            for k in range(TOPK):
                for t in range(NT):
                    eng.indirect_dma_start(out=slot_tok_d, out_offset=bass.IndirectOffsetOnAxis(
                        ap=slot[:, k, t:t + 1], axis=0), in_=token[:, t:t + 1], in_offset=None).then_inc(scattered, 16)
            eng.wait_ge(scattered, 16 * TOPK * NT)
            eng.dma_start(table[:], slot_tok_d.rearrange("(c p) o -> c (p o)", p=P)).then_inc(table_in, 16)
            eng.wait_ge(table_in, 16)

        def act(eng):
            nc.scalar.activation(probs[:], logits[:], ACT.Tanh, scale=1.0 / SOFTCAP).then_inc(tanh_done, 1)
            eng.wait_ge(exp_ready, 1)
            nc.scalar.activation(probs[:], work[:], ACT.Exp, scale=SOFTCAP).then_inc(exp_done0, 1)

        def pe(eng):
            eng.wait_ge(ahead_done, 1)
            flat = ahead[:].rearrange("p t e -> p (t e)")
            eng.matmul(rank_ps[:], before_b[:], chosen[:].rearrange("p t e -> p (t e)"), start=True, stop=False)
            eng.matmul(rank_ps[:], ones_b[:], flat[:, 0:NT * EXPERTS], start=False, stop=True)
            eng.matmul(count_ps[:], ones_b[:], flat[:, NT * EXPERTS:], start=True, stop=True).then_inc(rank_done, 1)
            eng.wait_ge(table_in, 16)
            eng.transpose(table_ps[:], table[:], ident[0:SC, 0:SC]).then_inc(table_t, 1)

        def dve(eng):
            link = chain(eng, r_step, 0)

            def over_e(ap):
                return ap.unsqueeze(2).to_broadcast(shape)

            eng.wait_ge(tanh_done, 1)
            link(eng.tensor_reduce(row[:], probs[:], AX, ALU.max))
            eng.tensor_tensor(work[:], probs[:], over_e(row[:]), ALU.subtract).then_inc(exp_ready, 1)
            eng.wait_ge(exp_done0, 1)
            link(eng.tensor_reduce(row[:], probs[:], AX, ALU.add))
            link(eng.reciprocal(row[:], row[:]))
            link(eng.tensor_tensor(probs[:], probs[:], over_e(row[:]), ALU.mult))
            eng.wait_ge(iota_done, 1)
            for k in range(TOPK):
                link(eng.tensor_reduce(slot_w[:, k, :], probs[:], AX, ALU.max))
                link(eng.tensor_tensor(work[:], probs[:], over_e(slot_w[:, k, :]), ALU.is_equal))
                link(eng.scalar_tensor_tensor(work[:], work[:], -float(EXPERTS), e_iota[:], ALU.mult, ALU.add))
                link(eng.tensor_reduce(row[:], work[:], AX, ALU.min))
                link(eng.tensor_tensor(picked[k][:], e_below[:], over_e(row[:]), ALU.is_equal))
                if k == 0:
                    link(eng.scalar_tensor_tensor(probs[:], picked[0][:], -2.0, probs[:], ALU.mult, ALU.add))
            link(eng.tensor_tensor(chosen[:], picked[0][:], picked[1][:], ALU.add))
            link(eng.memset(ahead[:, 0, :], 0.0))
            for t in range(NT):
                link(eng.tensor_tensor(ahead[:, t + 1, :], ahead[:, t, :], chosen[:, t, :], ALU.add))
            eng.nop().then_inc(ahead_done, 1)
            eng.wait_ge(rank_done, 1)
            e2 = [P, EXPERTS, EXPERTS]
            link(eng.tensor_copy(ntile[:], count_ps[:]))
            link(eng.tensor_tensor(steps[:], ntile[:].unsqueeze(2).to_broadcast(e2), steps[:], ALU.is_gt))
            link(eng.tensor_reduce(ntile[:], steps[:], AX, ALU.add))
            link(eng.tensor_copy(upto[:, 0:1], ntile[:, 0:1]))
            for e in range(1, EXPERTS):
                link(eng.tensor_tensor(upto[:, e:e + 1], upto[:, e - 1:e], ntile[:, e:e + 1], ALU.add))
            link(eng.tensor_tensor(base[:], upto[:], ntile[:], ALU.subtract))
            link(eng.tensor_scalar(base[:], base[:], float(SLOTS), None, ALU.mult))
            link(eng.tensor_tensor(work[:], rank_ps[:].rearrange("p (t e) -> p t e", e=EXPERTS),
                                   base[:].unsqueeze(1).to_broadcast(shape), ALU.add))
            for k in range(TOPK):
                link(eng.tensor_tensor(picked[k][:], picked[k][:], work[:], ALU.mult))
                link(eng.tensor_reduce(slot_f[:, k, :], picked[k][:], AX, ALU.add))
            eng.tensor_copy(slot[:], slot_f[:]).then_inc(slot_done, 1)
            ts = [P, TILES + 1, EXPERTS]
            link(eng.tensor_tensor(tile_w[:], tile_i[:], upto[:].unsqueeze(1).to_broadcast(ts), ALU.is_ge))
            link(eng.tensor_reduce(tile_f[:], tile_w[:], AX, ALU.add))
            link(eng.tensor_scalar(tile_f[:], tile_f[:], float(EXPERTS - 1), None, ALU.min))
            eng.tensor_copy(tile_expert[:], tile_f[:]).then_inc(token_done, 1)
            eng.wait_ge(table_t, 1)
            eng.tensor_copy(slot_token[:], table_ps[:]).then_inc(token_done, 1)

        return dict(sp=lambda eng: None, pool=pool, act=act, dve=dve, pe=pe)

    def expert_stage():
        st = ExitStack()
        raw = sb(st, "w_raw", [P, 2, CHW])
        whi = sb(st, "w_hi", [P, CH, CHW], F32R)
        wlo = sb(st, "w_lo", [P, CH, CHW], F32R)
        xg = sb(st, "x_rows", [P, 2, D])
        xidx = sb(st, "x_idx", [P, 2], I32)
        xth = sb(st, "xs_hi", [P, KC, SLOTS], F32R)
        xtl = sb(st, "xs_lo", [P, KC, SLOTS], F32R)
        sg = sb(st, "silu", [P, 2, CSUB * SLOTS])
        hh = sb(st, "h", [P, 2, CSUB * SLOTS])
        hhi = sb(st, "h_hi", [P, 2, CSUB * SLOTS], F32R)
        hlo = sb(st, "h_lo", [P, 2, CSUB * SLOTS], F32R)
        ysb = sb(st, "y_rows", [P, 2, D])
        up_ps = [[ps(st, f"up{w}_{q}", [P, CSUB * SLOTS]) for w in (1, 3)] for q in range(2)]
        y_ps = ps(st, "y_ps", [P, 2, D])
        x_ps = ps(st, "x_ps", [P, KC, SLOTS])
        st.close()
        w_in = [sem(f"w_in{r}") for r in range(2)]
        whi_done, wlo_done = sem("whi_done"), sem("wlo_done")
        idx_done, x_in, xs_t, xsh_done, xsl_done = (sem(n) for n in ("xidx_done", "xrows_in", "xs_t", "xsh_done", "xsl_done"))
        up_done, silu_done, gated, h_hi_done, h_done = (sem(n) for n in ("up_done", "silu_done", "gated", "h_hi_done", "h_done"))
        used, y_copied, y_stored = (sem(n) for n in ("chunk_used", "y_copied", "y_stored"))

        w1_c = w1.rearrange("e (k p) i -> e p k i", p=P)
        w3_c = w3.rearrange("e (k p) i -> e p k i", p=P)
        w2_c = w2.rearrange("e (c s p) d -> e c p s d", c=CH, p=P)
        y_t = y_d.rearrange("(i h p) d -> i p h d", h=2, p=P)

        def sp(eng):
            def turn(i, first):
                e = eng.value_load(tile_expert[0:1, bass.ds(i, 1)], min_val=0, max_val=EXPERTS - 1)
                for c in range(CH):
                    r = c % 2
                    if not first or c >= 2:
                        eng.wait_ge(wlo_done, CH * i + c - 1)
                    for n, w in enumerate((w1_c, w3_c)):
                        eng.dma_start(raw[:, r, n * UPW:(n + 1) * UPW].rearrange("p (k j) -> p k j", k=KC),
                                      one(w, e, "a p k i -> (a p) k i")[:, :, c * CW:(c + 1) * CW]).then_inc(w_in[r], 16)
                    eng.dma_start(raw[:, r, 2 * UPW:CHW].rearrange("p (s d) -> p s d", s=CSUB),
                                  one(w2_c, e, "a c p s d -> (a c) p s d")[c]).then_inc(w_in[r], 16)
            repeat(eng, TILES, turn)

        def pool(eng):
            def turn(i, first):
                if not first:
                    eng.wait_ge(xs_t, i)
                eng.tensor_copy(xidx[:], slot_token[:, bass.ds(2 * i, 2)]).then_inc(idx_done, 1)
                eng.wait_ge(idx_done, i + 1)
                settle(eng)
                for h in range(2):
                    eng.indirect_dma_start(out=xg[:, h, :], out_offset=None, in_=xn_d,
                                           in_offset=bass.IndirectOffsetOnAxis(ap=xidx[:, h:h + 1], axis=0)
                                           ).then_inc(x_in, 16)
                eng.wait_ge(x_in, 32 * i + 32)
            repeat(eng, TILES, turn)

        def act(eng):
            def split(i, c):
                g, s, r = CH * i + c, c % CH, c % 2
                eng.wait_ge(w_in[r], 48 * (2 * i + c // 2 + 1))
                if not (isinstance(g, int) and g < CH):
                    eng.wait_ge(used, g - CH + 1)
                nc.scalar.copy(whi[:, s, :], raw[:, r, :]).then_inc(whi_done, 1)

            def xs_hi(i):
                eng.wait_ge(xs_t, i + 1)
                nc.scalar.copy(xth[:], x_ps[:]).then_inc(xsh_done, 1)

            def turn(i, first, last=False):
                for c in range(CH):
                    g = CH * i + c
                    if c == CH - 1 and not last:
                        xs_hi(i + 1)
                    eng.wait_ge(up_done, g + 1)
                    if not (first and c < 2):
                        eng.wait_ge(gated, g - 1)
                    nc.scalar.activation(sg[:, c % 2, :], up_ps[c % 2][0][:], ACT.Silu).then_inc(silu_done, 1)
                    if c == 0 and not first:
                        y_rows(i - 1, first=False)
                    if not (last and c >= 2):
                        split(i, c + 2)

            def y_rows(i, first):
                eng.wait_ge(used, CH * i + CH)
                nc.scalar.copy(ysb[:], y_ps[:]).then_inc(y_copied, 1)
                eng.wait_ge(y_copied, i + 1)
                eng.dma_start(one(y_t, i, "a p h d -> (a p) h d"), ysb[:]).then_inc(y_stored, 16)

            split(0, 0)
            split(0, 1)
            xs_hi(0)
            turn(0, True)
            with eng.Fori(1, TILES - 1) as i:
                turn(i, False)
                eng.wait_ge(y_stored, 16 * i)
            turn(TILES - 1, False, last=True)
            eng.wait_ge(y_stored, 16 * (TILES - 1))
            y_rows(TILES - 1, first=False)
            eng.wait_ge(y_stored, 16 * TILES)

        def dve(eng):
            def split(i, c):
                g, s, r = CH * i + c, c % CH, c % 2
                eng.wait_ge(whi_done, g + 1)
                eng.tensor_tensor(wlo[:, s, :], raw[:, r, :], whi[:, s, :].bitcast(F32), ALU.subtract).then_inc(wlo_done, 1)

            def xs_lo(i):
                eng.wait_ge(xsh_done, i + 1)
                eng.tensor_tensor(xtl[:], x_ps[:], xth[:].bitcast(F32), ALU.subtract).then_inc(xsl_done, 1)

            def turn(i, first, last=False):
                for c in range(CH):
                    g = CH * i + c
                    if c == CH - 1 and not last:
                        xs_lo(i + 1)
                    eng.wait_ge(silu_done, g + 1)
                    if not (first and c < 2):
                        eng.wait_ge(h_done, g - 1)
                    eng.tensor_tensor(hh[:, c % 2, :], sg[:, c % 2, :], up_ps[c % 2][1][:], ALU.mult).then_inc(gated, 1)
                    eng.wait_ge(gated, g + 1)
                    if not (first and c < 2):
                        eng.wait_ge(used, g - 1)
                    eng.tensor_copy(hhi[:, c % 2, :], hh[:, c % 2, :]).then_inc(h_hi_done, 1)
                    eng.wait_ge(h_hi_done, g + 1)
                    eng.tensor_tensor(hlo[:, c % 2, :], hh[:, c % 2, :], hhi[:, c % 2, :].bitcast(F32), ALU.subtract).then_inc(h_done, 1)
                    if not (last and c >= 2):
                        split(i, c + 2)
            split(0, 0)
            split(0, 1)
            xs_lo(0)
            turn(0, True)
            with eng.Fori(1, TILES - 1) as i:
                turn(i, False)
            turn(TILES - 1, False, last=True)

        def pe(eng):
            def rows_t(i, first):
                eng.wait_ge(x_in, 32 * i + 32)
                if not first:
                    eng.wait_ge(xsl_done, i)
                for k in range(KC):
                    for h in range(2):
                        last = eng.transpose(x_ps[:, k, h * P:(h + 1) * P], xg[:, h, k * P:(k + 1) * P], ident[:])
                last.then_inc(xs_t, 1)

            def up(i, c, first):
                g, s, q = CH * i + c, c % CH, c % 2
                eng.wait_ge(wlo_done, g + 1)
                if c == 0:
                    eng.wait_ge(xsl_done, i + 1)
                if not (first and c < 2):
                    eng.wait_ge(gated, g - 1)
                for n in range(2):
                    for j in range(CSUB):
                        step = 0
                        for k in range(KC):
                            at = slice(n * UPW + k * CW + j * P, n * UPW + k * CW + (j + 1) * P)
                            for w, v in ((whi, xth), (whi, xtl), (wlo, xth)):
                                last = eng.matmul(up_ps[q][n][:, j * SLOTS:(j + 1) * SLOTS], w[:, s, at], v[:, k, :],
                                                  start=(step == 0), stop=(step == 3 * KC - 1))
                                step += 1
                last.then_inc(up_done, 1)

            def down(i, c, first):
                g, q = CH * i + c, c % 2
                eng.wait_ge(h_done, g + 1)
                if c == 0 and not first:
                    eng.wait_ge(y_copied, i)
                for h in range(2):
                    step = 0
                    for j in range(CSUB):
                        at = slice(j * SLOTS + h * P, j * SLOTS + (h + 1) * P)
                        wat = slice(2 * UPW + j * D, 2 * UPW + (j + 1) * D)
                        for v, w in ((hhi, whi), (hhi, wlo), (hlo, whi)):
                            last = eng.matmul(y_ps[:, h, :], v[:, q, at], w[:, c, wat],
                                              start=(c == 0 and step == 0), stop=(c == CH - 1 and step == 3 * CSUB - 1))
                            step += 1
                last.then_inc(used, 1)

            def turn(i, first, last=False):
                up(i, 1, first)
                down(i, 0, first)
                up(i, 2, first)
                down(i, 1, first)
                up(i, 3, first)
                if not last:
                    rows_t(i + 1, False)
                down(i, 2, first)
                if not last:
                    up(i + 1, 0, False)
                down(i, 3, first)

            rows_t(0, True)
            up(0, 0, True)
            turn(0, True)
            with eng.Fori(1, TILES - 1) as i:
                turn(i, False)
            turn(TILES - 1, False, last=True)

        return dict(sp=sp, pool=pool, act=act, dve=dve, pe=pe)

    def mlp_stage():
        st = ExitStack()
        yg = sb(st, "y_gathered", [P, TOPK, RT, D])
        yidx = sb(st, "y_idx", [P, TOPK, RT], I32)
        yw = sb(st, "y_w", [P, TOPK, RT])
        x1 = sb(st, "x1", [P, RT, D])
        xn = sb(st, "x1n", [P, RT, D])
        ln = norm_buffers(st, "ln1")
        xth = sb(st, "x1t_hi", [P, KC, SEQ], F32R)
        xtl = sb(st, "x1t_lo", [P, KC, SEQ], F32R)
        relu = sb(st, "relu", [P, 2, SEQ])
        sq = sb(st, "relu2", [P, 2, SEQ])
        hhi = sb(st, "relu2_hi", [P, 2, SEQ], F32R)
        hlo = sb(st, "relu2_lo", [P, 2, SEQ], F32R)
        res = sb(st, "layer_sum", [P, RT, D])
        xt_ps = [ps(st, f"x1t_ps{i}", [P, SEQ]) for i in range(2)]
        h_ps = [ps(st, f"hid_ps{i}", [P, SEQ]) for i in range(2)]
        y_ps = ps(st, "mlp_ps", [P, RT, D])
        st.close()
        r0_in, idx_done, yg_in = sem("r0_in"), sem("yidx_done"), sem("yg_in")
        yw_done, mixed = sem("yw_done"), sem("mixed")
        ln_step, sqrt_done, xn_ready = sem("ln1_step"), sem("ln1_sqrt_done"), sem("x1n_ready")
        xt_done, xth_done, xtl_done, xt_stored = (sem(n) for n in ("x1t_done", "x1th_done", "x1tl_done", "x1t_stored"))
        hid_done, relu_done, sq_done, hhi_done, hlo_done = (
            sem(n) for n in ("hid_done", "relu_done", "sq_done", "hhi_done", "hlo_done"))
        mlp_used, res_done, res_stored = sem("mlp_used"), sem("res_done"), sem("res_stored")

        r0_b = r0_d.rearrange("(b t p) d -> b p t d", b=BATCH, p=P)
        r1_b = r1_d.rearrange("(b t p) d -> b p t d", b=BATCH, p=P)

        def sp(eng):
            def turn(b, first):
                if not first:
                    eng.wait_ge(res_done, b)
                eng.dma_start(x1[:], one(r0_b, b, "a p t d -> (a p) t d")).then_inc(r0_in, 16)
                eng.wait_ge(xtl_done, KC * b + KC)
                for s, t in enumerate((xth, xtl)):
                    eng.dma_start(one(xt1_d[s], b, "a p n -> (a p) n"),
                                  t[:].bitcast(F32).rearrange("p k n -> p (k n)")).then_inc(xt_stored, 16)
                eng.wait_ge(res_done, b + 1)
                eng.dma_start(one(r1_b, b, "a p t d -> (a p) t d"), res[:]).then_inc(res_stored, 16)
            repeat(eng, BATCH, turn)
            eng.wait_ge(xt_stored, 32 * BATCH)
            eng.wait_ge(res_stored, 16 * BATCH)

        def pool(eng):
            def turn(b, first):
                eng.tensor_copy(yidx[:], slot[:, :, bass.ds(RT * b, RT)]).then_inc(idx_done, 1)
                eng.wait_ge(idx_done, b + 1)
                if not first:
                    eng.wait_ge(mixed, 2 * b)
                    settle(eng)
                for k in range(TOPK):
                    for t in range(RT):
                        eng.indirect_dma_start(out=yg[:, k, t, :], out_offset=None, in_=y_d,
                                               in_offset=bass.IndirectOffsetOnAxis(ap=yidx[:, k, t:t + 1], axis=0)
                                               ).then_inc(yg_in, 16)
                for m in range(HM):
                    q = m % 2
                    eng.wait_ge(relu_done, HM * b + m + 1)
                    if not (first and m < 2):
                        eng.wait_ge(hlo_done, HM * b + m - 1)
                    eng.tensor_tensor(sq[:, q, :], relu[:, q, :], relu[:, q, :], ALU.mult).then_inc(sq_done, 1)
                eng.wait_ge(yg_in, 16 * TOPK * RT * (b + 1))
            repeat(eng, BATCH, turn)

        def act(eng):
            def turn(b, first):
                eng.wait_ge(ln_step, LN_STEPS * b + 3)
                nc.scalar.activation(ln["rstd"][:], ln["var"][:], ACT.Sqrt).then_inc(sqrt_done, 1)
                if not first:
                    eng.wait_ge(xt_stored, 32 * b)
                for k in range(KC):
                    eng.wait_ge(xt_done, KC * b + k + 1)
                    nc.scalar.copy(xth[:, k, :], xt_ps[k % 2][:]).then_inc(xth_done, 1)
                for m in range(HM):
                    q, g = m % 2, HM * b + m
                    eng.wait_ge(hid_done, g + 1)
                    if not (first and m < 2):
                        eng.wait_ge(sq_done, g - 1)
                        eng.wait_ge(mlp_used, g - 1)
                    nc.scalar.activation(relu[:, q, :], h_ps[q][:], ACT.Relu, scale=fc_scale[:, 0:1]).then_inc(relu_done, 1)
                    eng.wait_ge(relu_done, g + 1)
                    nc.scalar.activation(hhi[:, q, :], relu[:, q, :], ACT.Square).then_inc(hhi_done, 1)
            repeat(eng, BATCH, turn)

        def dve(eng):
            def turn(b, first):
                eng.tensor_copy(yw[:], slot_w[:, :, bass.ds(RT * b, RT)]).then_inc(yw_done, 1)
                eng.wait_ge(yw_done, b + 1)
                eng.wait_ge(r0_in, 16 * b + 16)
                eng.wait_ge(yg_in, 16 * TOPK * RT * (b + 1))
                for k in range(TOPK):
                    for t in range(RT):
                        last = eng.scalar_tensor_tensor(x1[:, t, :], yg[:, k, t, :], yw[:, k, t:t + 1], x1[:, t, :],
                                                        ALU.mult, ALU.add)
                    last.then_inc(mixed, 1)
                    eng.wait_ge(mixed, 2 * b + k + 1)
                layer_norm(eng, x1, ln, ln_step, LN_STEPS * b, sqrt_done, b + 1)
                normed(eng, x1, xn, ln).then_inc(xn_ready, 1)
                if not first:
                    eng.wait_ge(xt_stored, 32 * b)
                for k in range(KC):
                    eng.wait_ge(xth_done, KC * b + k + 1)
                    eng.tensor_tensor(xtl[:, k, :], xt_ps[k % 2][:], xth[:, k, :].bitcast(F32),
                                      ALU.subtract).then_inc(xtl_done, 1)
                for m in range(HM):
                    q, g = m % 2, HM * b + m
                    eng.wait_ge(sq_done, g + 1)
                    eng.wait_ge(hhi_done, g + 1)
                    if not (first and m < 2):
                        eng.wait_ge(mlp_used, g - 1)
                    eng.tensor_tensor(hlo[:, q, :], sq[:, q, :], hhi[:, q, :].bitcast(F32), ALU.subtract).then_inc(hlo_done, 1)
                if not first:
                    eng.wait_ge(res_stored, 16 * b)
                eng.wait_ge(mlp_used, HM * b + HM)
                for t in range(RT):
                    last = eng.scalar_tensor_tensor(res[:, t, :], y_ps[:, t, :], proj_scale[:, 0:1], x1[:, t, :],
                                                    ALU.mult, ALU.add)
                last.then_inc(res_done, 1)
            repeat(eng, BATCH, turn)

        def pe(eng):
            def turn(b, first):
                eng.wait_ge(xn_ready, b + 1)
                for k in range(KC):
                    if not (first and k < 2):
                        eng.wait_ge(xtl_done, KC * b + k - 1)
                    for t in range(RT):
                        last = eng.transpose(xt_ps[k % 2][:, t * P:(t + 1) * P], xn[:, t, k * P:(k + 1) * P], ident[:])
                    last.then_inc(xt_done, 1)

                def hidden(m):
                    q, g = m % 2, HM * b + m
                    if not (first and m < 2):
                        eng.wait_ge(relu_done, g - 1)
                    for k in range(KC):
                        if m == 0:
                            eng.wait_ge(xtl_done, KC * b + k + 1)
                        for v in (xth, xtl):
                            last = eng.matmul(h_ps[q][:], fcT[:, k, m * P:(m + 1) * P], v[:, k, :],
                                              start=(k == 0 and v is xth), stop=(k == KC - 1 and v is xtl))
                    last.then_inc(hid_done, 1)

                hidden(0)
                for m in range(HM):
                    q = m % 2
                    if m + 1 < HM:
                        hidden(m + 1)
                    eng.wait_ge(hlo_done, HM * b + m + 1)
                    if m == 0 and not first:
                        eng.wait_ge(res_done, b)
                    for t in range(RT):
                        for h in (hhi, hlo):
                            last = eng.matmul(y_ps[:, t, :], h[:, q, t * P:(t + 1) * P], projT[:, m, :],
                                              start=(m == 0 and h is hhi), stop=(m == HM - 1 and h is hlo))
                    last.then_inc(mlp_used, 1)
            repeat(eng, BATCH, turn)

        return dict(sp=sp, pool=pool, act=act, dve=dve, pe=pe)

    def rows(ap):
        return ap.rearrange("(k p) n -> p k n", p=P)

    def weights0_stage(W):
        st = ExitStack()
        G = 4
        rq = sb(st, "wq_raw", [P, KC, D])
        rk = sb(st, "wk_raw", [P, KC, P])
        rv = sb(st, "wv_raw", [P, KC, P])
        rwo = sb(st, "wo_raw", [P, D])
        qsum = sb(st, "q_sum", [P, KC, P])
        braw = sb(st, "b_raw", [1, D + 2 * P])
        bor = sb(st, "bo_raw", [1, D])
        bsum = sb(st, "bq_sum", [1, P])
        st.close()
        w_in0, w_step = sem("w0_in"), sem("w0_step")

        def sp(eng):
            eng.dma_start(rq[:], rows(wq)).then_inc(w_in0, 16)
            eng.dma_start(rk[:], rows(wk)).then_inc(w_in0, 16)
            eng.dma_start(rv[:], rows(wv)).then_inc(w_in0, 16)
            eng.dma_start(rwo[:], wo).then_inc(w_in0, 16)
            row = "(o n) -> o n"
            eng.dma_start(braw[:, 0:D], bq.rearrange(row, o=1)).then_inc(w_in0, 16)
            eng.dma_start(braw[:, D:D + P], bk.rearrange(row, o=1)).then_inc(w_in0, 16)
            eng.dma_start(braw[:, D + P:], bv.rearrange(row, o=1)).then_inc(w_in0, 16)
            eng.dma_start(bor[:], bo.rearrange(row, o=1)).then_inc(w_in0, 16)
            eng.dma_start(W["cos"][:], cos).then_inc(w_in0, 16)
            eng.dma_start(W["sin"][:], sin).then_inc(w_in0, 16)

        def dve(eng):
            link = chain(eng, w_step, 0)
            eng.wait_ge(w_in0, 160)
            for r, s in ((rq[:].rearrange("p k n -> p (k n)"), qsum[:].rearrange("p k n -> p (k n)")),
                         (braw[:, 0:D], bsum[:])):
                heads = r.rearrange("p (h g d) -> p h g d", g=G, d=HD)
                total = s.rearrange("p (h d) -> p h d", d=HD)
                link(eng.tensor_tensor(total, heads[:, :, 0, :], heads[:, :, 1, :], ALU.add))
                for g in (2, 3):
                    link(eng.tensor_tensor(total, total, heads[:, :, g, :], ALU.add))

            def split_turned(src, name):
                a_hi, a_lo, b_hi, b_lo = (W[f"{name}{v}_{s}"] for v in "AB" for s in ("hi", "lo"))

                def halves(t):
                    flat = t[:].rearrange("p k n -> p (k n)") if len(t.shape) == 3 else t[:]
                    return flat.rearrange("p (h two i) -> p h two i", two=2, i=HD // 2)
                pairs = src.rearrange("p (h i two) -> p h two i", two=2, i=HD // 2)
                link(eng.tensor_copy(halves(a_hi), pairs))
                link(eng.tensor_tensor(halves(a_lo), pairs, halves(a_hi).bitcast(F32), ALU.subtract))
                for a, b in ((a_hi, b_hi), (a_lo, b_lo)):
                    a, b = halves(a), halves(b)
                    link(eng.tensor_scalar(b[:, :, 0, :], a[:, :, 1, :].bitcast(F32), -1.0, None, ALU.mult))
                    link(eng.tensor_copy(b[:, :, 1, :], a[:, :, 0, :].bitcast(F32)))

            def split(src, hi, lo):
                link(eng.tensor_copy(hi, src))
                link(eng.tensor_tensor(lo, src, hi.bitcast(F32), ALU.subtract))

            split_turned(qsum[:].rearrange("p k n -> p (k n)"), "q")
            split_turned(rk[:].rearrange("p k n -> p (k n)"), "k")
            split_turned(bsum[:], "bq")
            split_turned(braw[:, D:D + P], "bk")
            split(rv[:], W["v_hi"][:], W["v_lo"][:])
            split(braw[:, D + P:], W["bv_hi"][:], W["bv_lo"][:])
            split(rwo[:], W["o_hi"][:, 0, :], W["o_lo"][:, 0, :])
            split(bor[:], W["bo_hi"][:], W["bo_lo"][:])
            link(eng.tensor_copy(W["ones_r"][:], ones[0:1, 0:1].to_broadcast([1, SEQ])))

        return dict(sp=sp, dve=dve, pool=lambda e: None, act=lambda e: None, pe=lambda e: None)

    def weights1_stage(W):
        st = ExitStack()
        raw = sb(st, "w1_raw", [P, KC, 4 * D])
        st.close()
        w_in1, w_hi, w_lo = sem("w1a_in"), sem("w1a_hi"), sem("w1a_lo")

        def sp(eng):
            eng.dma_start(raw[:, :, 0:3 * D], rows(w_qkv)).then_inc(w_in1, 16)
            eng.dma_start(raw[:, :, 3 * D:], rows(w_out)).then_inc(w_in1, 16)

        def act(eng):
            eng.wait_ge(w_in1, 32)
            for k in range(KC):
                nc.scalar.copy(W["hi"][:, k, :], raw[:, k, :]).then_inc(w_hi, 1)

        def dve(eng):
            for k in range(KC):
                eng.wait_ge(w_hi, k + 1)
                last = eng.tensor_tensor(W["lo"][:, k, :], raw[:, k, :], W["hi"][:, k, :].bitcast(F32), ALU.subtract)
            last.then_inc(w_lo, 1)
        return dict(sp=sp, act=act, dve=dve, pool=lambda e: None, pe=lambda e: None)

    WIDTH = [P * (i + 1) for i in range(RT)]
    ORDER = [3, 2, 0, 1]
    BANK_END = [0, 2, 2, 3]
    S_AT = [896, 1024, 512, 0]
    T_WIDTH = [SEQ - P * k for k in range(RT)]
    T_AT = [0, 512, 1024, 896]
    TRI = sum(WIDTH)

    def attention_stage(L, W, V_strip, groups, per_body, per_batch, rotated, xt_d, res_d, dst_d):
        NH = 4 * groups
        HB = 4 * per_body
        bodies = groups // per_body
        batches_per_body = per_body // per_batch if per_body >= per_batch else 1
        VW = P * per_batch
        XB = 2 if per_batch == 1 else 1
        n_ = lambda t: f"{t}_{L}"
        st = ExitStack()
        xth = sb(st, n_("axt_hi"), [P, XB, KC, SEQ], F32R)
        xtl = sb(st, n_("axt_lo"), [P, XB, KC, SEQ], F32R)
        qh, ql, kh, kl = (sb(st, n_(t), [P, 2, SEQ], F32R) for t in ("q_hi", "q_lo", "k_hi", "k_lo"))
        vf = sb(st, n_("v"), [P, RT, VW])
        vh, vl = V_strip
        probs = sb(st, n_("p"), [P, 2, TRI])
        pth = sb(st, n_("pt_hi"), [P, 2, TRI], F32R)
        ptl = sb(st, n_("pt_lo"), [P, 2, TRI], F32R)
        nmax = sb(st, n_("nmax"), [P, 2, RT])
        rsum = sb(st, n_("rsum"), [P, 2, RT])
        rinv = sb(st, n_("rinv"), [P, 2, RT])
        oth = sb(st, n_("ot_hi"), [P, per_batch, SEQ], F32R)
        otl = sb(st, n_("ot_lo"), [P, per_batch, SEQ], F32R)
        res = sb(st, n_("res"), [P, 2, D])
        osb = sb(st, n_("osb"), [P, 2, D])
        if rotated:
            ra, rb, rot = (sb(st, n_(t), [P, SEQ]) for t in ("ra", "rb", "rot"))
        s_ps = ps(st, n_("s_ps"), [P, 3 * SEQ])
        t_ps = ps(st, n_("t_ps"), [P, 3 * SEQ])
        o_ps = ps(st, n_("o_ps"), [P, SEQ])
        pj = ps(st, n_("pj"), [P, SEQ])
        st.close()
        (s_done, max_done, exp_done, rinv_done, norm_done, t_done, th_done, tl_done, pv_done, oh_done, ol_done,
         vh_done, vl_done, pj_done, pj_free, qh_done, ql_done, ro_done) = (sem(n_(t)) for t in (
             "s_done", "max_done", "exp_done", "rinv_done", "norm_done", "t_done", "th_done", "tl_done", "pv_done",
             "oh_done", "ol_done", "vh_done", "vl_done", "pj_done", "pj_free", "qh_done", "ql_done", "ro_done"))
        xt_in = [sem(n_(f"axt_in{i}")) for i in range(XB)]
        res_in = [sem(n_(f"res_in{i}")) for i in range(2)]
        stored = [sem(n_(f"stored{i}")) for i in range(2)]

        def jobs(s):
            out_ = []
            for back, parts in ((7, (0, 1)), (8, (2,)), (9, (3,))):
                g, left = divmod(s - back, 4)
                if left == 0 and 0 <= g < groups and (g + 1) % per_batch == 0:
                    out_ += [("out", g, t) for t in parts]
            g, j = s // 4 + 1, s % 4
            if 0 <= g < groups:
                fresh = g % per_batch == 0
                if rotated:
                    out_ += {0: [], 1: [("qA", g, 0), ("qB", g, 0)], 2: [("kA", g, 0), ("kB", g, 0)],
                             3: [("v", g, t) for t in range(RT)]}[j]
                else:
                    out_ += {0: [("q", g, 0)], 1: [("k", g, 0)], 2: [("v", g, 0), ("v", g, 1)] if fresh else [],
                             3: [("v", g, 2), ("v", g, 3)] if fresh else []}[j]
            return out_

        number = {}
        for s in range(-4, NH + 6):
            for job in jobs(s):
                number[job] = len(number)
        uses = sum(len(jobs(s)) for s in range(HB, 2 * HB))

        class At:
            def __init__(self, i=None):
                self.i = i

            def __call__(self, value, per_body_):
                return value if self.i is None else value + per_body_ * (self.i - 1)

            def heads(self, v):
                return self(v, HB)

            def tiles(self, v):
                return self(v, RT * HB)

            def groups(self, v, times=1):
                return self(v, times * per_body)

            def jobs(self, v):
                return self(v, uses)

            def batches(self, v, times=1):
                return self(v, times * batches_per_body)

        def run(eng, step):
            for s in range(-4, HB):
                step(eng, s, At())
            if bodies > 2:
                with eng.Fori(1, bodies - 1) as i:
                    for s in range(HB, 2 * HB):
                        step(eng, s, At(i))
            for s in range(HB * (bodies - 1), NH + 6):
                step(eng, s, At())

        def last_out(g):
            before = ("out", g // per_batch * per_batch - 1, RT - 1)
            return number.get(before)

        def pe_step(eng, s, at):
            if 0 <= s < NH:
                g, j = divmod(s, 4)
                if j == 0:
                    if rotated:
                        eng.wait_ge(ql_done, at.groups(2 * g + 2, 2))
                    else:
                        eng.wait_ge(pj_free, at.jobs(number[("k", g, 0)] + 1))
                if s:
                    eng.wait_ge(exp_done, at.tiles(RT * s))
                r = slice(HD * j, HD * (j + 1))
                for i in ORDER:
                    o = s_ps[:, S_AT[i]:S_AT[i] + WIDTH[i]]
                    for n, (a, b) in enumerate(((qh, kh), (qh, kl), (ql, kh))):
                        eng.matmul(o, a[r, g % 2, i * P:(i + 1) * P], b[r, g % 2, 0:WIDTH[i]], start=(n == 0), stop=False)
                    eng.matmul(s_ps[:, S_AT[i] + i * P:S_AT[i] + (i + 1) * P], ident_b[:], mask_b[:],
                               start=False, stop=True).then_inc(s_done, 1)
            m = s - 1
            if 0 <= m < NH:
                eng.wait_ge(norm_done, at.heads(m + 1))
                if m:
                    eng.wait_ge(tl_done, at.heads(m))
                for k in range(RT):
                    for i in range(k, RT):
                        last = eng.transpose(t_ps[:, T_AT[k] + (i - k) * P:T_AT[k] + (i - k + 1) * P],
                                             probs[:, m % 2, S_AT[i] + k * P:S_AT[i] + (k + 1) * P], ident[:])
                last.then_inc(t_done, 1)
            m = s - 2
            if 0 <= m < NH:
                g, j = divmod(m, 4)
                eng.wait_ge(tl_done, at.heads(m + 1))
                if j == 0 and g:
                    eng.wait_ge(ol_done, at.groups(g))
                if j % 2 == 0:
                    eng.wait_ge(vl_done, at.groups(2 * g + j // 2 + 1, 2))
                for k in range(RT):
                    o = o_ps[:, k * P:SEQ]
                    c = slice(T_AT[k], T_AT[k] + T_WIDTH[k])
                    for n, (a, b) in enumerate(((vh, pth), (vh, ptl), (vl, pth))):
                        last = eng.matmul(o, a[:, k, j * P:(j + 1) * P], b[:, m % 2, c],
                                          start=(j == 0 and k == 0 and n == 0), stop=(j == 3 and k == 3 and n == 2))
                last.then_inc(pv_done, 1)
            for job in jobs(s):
                what, g, t = job
                u = number[job]
                b = g // per_batch
                if u:
                    eng.wait_ge(pj_free, at.jobs(u))
                if what in ("q", "qA") and g % per_batch == 0:
                    eng.wait_ge(xt_in[b % XB], at.batches(32 * (b // XB + 1), 32 // XB))
                x_h, x_l = xth[:, b % XB], xtl[:, b % XB]
                if what == "out":
                    eng.wait_ge(ol_done, at.groups(g + 1))
                    c = slice(t * P, (t + 1) * P)
                    terms = [(a[:, k, c], w_[:, k, :]) for k in range(per_batch)
                             for a, w_ in ((oth, W["o_hi"]), (oth, W["o_lo"]), (otl, W["o_hi"]))]
                    if rotated:
                        terms += [(W["ones_r"][:, 0:P], W["bo_hi"][:]), (W["ones_r"][:, 0:P], W["bo_lo"][:])]
                    o = pj[:]
                elif what == "v":
                    c = slice(t * P, (t + 1) * P)
                    terms = [(a[:, k, c], w_[:, k, :]) for k in range(KC)
                             for a, w_ in ((x_h, W["v_hi"]), (x_h, W["v_lo"]), (x_l, W["v_hi"]))]
                    if rotated:
                        terms += [(W["ones_r"][:, 0:P], W["bv_hi"][:]), (W["ones_r"][:, 0:P], W["bv_lo"][:])]
                    o = pj[:, 0:VW]
                else:
                    w_hi, w_lo = W[what + "_hi"], W[what + "_lo"]
                    c = slice((g % per_batch) * P, (g % per_batch + 1) * P)
                    terms = [(w_[:, k, c], v[:, k, :]) for k in range(KC)
                             for w_, v in ((w_hi, x_h), (w_hi, x_l), (w_lo, x_h))]
                    if rotated:
                        terms += [(W["b" + what + "_hi"][:], W["ones_r"][:]), (W["b" + what + "_lo"][:], W["ones_r"][:])]
                    o = pj[:]
                for n, (a, b_) in enumerate(terms):
                    last = eng.matmul(o, a, b_, start=(n == 0), stop=(n == len(terms) - 1))
                last.then_inc(pj_done, 1)

        def strip(t, half):
            return t[:, :, 320 * half:320 * (half + 1)].rearrange("p k (j c) -> p k j c", j=2)[:, :, :, 0:HD]

        def v_of(g, half):
            c = (g % per_batch) * P + 2 * HD * half
            return vf[:, :, c:c + 2 * HD].rearrange("p k (j d) -> p k j d", j=2)

        def strips_due(s):
            if s % 2 == 0 and 0 <= s < NH:
                return s // 4, s % 4 // 2

        def scale_of(what):
            return HD ** -0.5 if what[0] == "q" else 1.0

        def act_step(eng, s, at):
            if 0 <= s < NH:
                q = s % 2
                if s >= 2:
                    eng.wait_ge(t_done, at.heads(s - 1))
                for n, i in enumerate(ORDER):
                    eng.wait_ge(max_done, at.tiles(RT * s + BANK_END[n] + 1))
                    c = slice(S_AT[i], S_AT[i] + WIDTH[i])
                    nc.scalar.activation(probs[:, q, c], s_ps[:, c], ACT.Exp, bias=nmax[:, q, i:i + 1],
                                         accum_out=rsum[:, q, i:i + 1]).then_inc(exp_done, 1)
            m = s - 1
            if 0 <= m < NH:
                eng.wait_ge(t_done, at.heads(m + 1))
                if m >= 2:
                    eng.wait_ge(pv_done, at.heads(m - 1))
                nc.scalar.copy(pth[:, m % 2, :], t_ps[:, 0:TRI]).then_inc(th_done, 1)
            if s % 4 == 2 and 0 <= s - 6 < NH:
                g = (s - 6) // 4
                eng.wait_ge(pv_done, at.heads(4 * g + 4))
                if last_out(g) is not None:
                    eng.wait_ge(pj_done, at.jobs(last_out(g) + 1))
                nc.scalar.copy(oth[:, g % per_batch, :], o_ps[:]).then_inc(oh_done, 1)
            if strips_due(s):
                g, half = strips_due(s)
                if half == 0:
                    b = g // per_batch
                    eng.wait_ge(pj_free, at.jobs(number[("v", b * per_batch, RT - 1)] + 1))
                if g:
                    eng.wait_ge(pv_done, at.heads(4 * g - 2 + 2 * half))
                nc.scalar.copy(strip(vh, half), v_of(g, half)).then_inc(vh_done, 1)
            for job in jobs(s):
                what, g, t = job
                dst = {"q": qh, "k": kh}.get(what[0])
                if dst is None or what.endswith("A"):
                    continue
                if what.endswith("B"):
                    eng.wait_ge(ro_done, at.groups(2 * g + (what[0] == "k") + 1, 2))
                else:
                    eng.wait_ge(pj_done, at.jobs(number[job] + 1))
                if g >= 2:
                    eng.wait_ge(s_done, at.tiles(RT * 4 * (g - 1)))
                nc.scalar.activation(dst[:, g % 2, :], rot[:] if rotated else pj[:], ACT.Copy,
                                     scale=scale_of(what)).then_inc(qh_done, 1)

        def dve_step(eng, s, at):
            if 0 <= s < NH:
                q = s % 2
                for n, i in enumerate(ORDER):
                    eng.wait_ge(s_done, at.tiles(RT * s + BANK_END[n] + 1))
                    eng.tensor_reduce(nmax[:, q, i:i + 1], s_ps[:, S_AT[i]:S_AT[i] + WIDTH[i]], AX, ALU.max,
                                      negate=True).then_inc(max_done, 1)
            m = s - 1
            if 0 <= m < NH:
                eng.wait_ge(th_done, at.heads(m + 1))
                if m >= 2:
                    eng.wait_ge(pv_done, at.heads(m - 1))
                eng.tensor_tensor(ptl[:, m % 2, :], t_ps[:, 0:TRI], pth[:, m % 2, :].bitcast(F32),
                                  ALU.subtract).then_inc(tl_done, 1)
            if 0 <= s < NH:
                eng.wait_ge(exp_done, at.tiles(RT * s + RT))
                eng.reciprocal(rinv[:, s % 2, :], rsum[:, s % 2, :]).then_inc(rinv_done, 1)
            if s % 4 == 2 and 0 <= s - 6 < NH:
                g = (s - 6) // 4
                eng.wait_ge(oh_done, at.groups(g + 1))
                eng.tensor_tensor(otl[:, g % per_batch, :], o_ps[:], oth[:, g % per_batch, :].bitcast(F32),
                                  ALU.subtract).then_inc(ol_done, 1)
            if strips_due(s):
                g, half = strips_due(s)
                eng.wait_ge(vh_done, at.groups(2 * g + half + 1, 2))
                eng.tensor_tensor(strip(vl, half), v_of(g, half), strip(vh, half).bitcast(F32),
                                  ALU.subtract).then_inc(vl_done, 1)
            for job in jobs(s):
                what, g, t = job
                u = number[job]
                b = g // per_batch
                if what == "v":
                    if g and t == 0:
                        eng.wait_ge(vl_done, at.groups(2 * g, 2))
                    eng.wait_ge(pj_done, at.jobs(u + 1))
                    eng.tensor_copy(vf[:, t, :], pj[:, 0:VW]).then_inc(pj_free, 1)
                elif what == "out":
                    eng.wait_ge(pj_done, at.jobs(u + 1))
                    eng.wait_ge(res_in[t % 2], at.batches(16 * (2 * b + t // 2 + 1), 32))
                    if b or t >= 2:
                        eng.wait_ge(stored[t % 2], at.batches(16 * (2 * b + t // 2), 32))
                    eng.tensor_tensor(osb[:, t % 2, :], pj[:], res[:, t % 2, :], ALU.add).then_inc(pj_free, 1)
                elif what.endswith("A"):
                    eng.wait_ge(pj_done, at.jobs(u + 1))
                    eng.tensor_tensor(ra[:], pj[:], W["cos"][:], ALU.mult).then_inc(pj_free, 1)
                else:
                    turn = 2 * g + (what[0] == "k") + 1
                    src = pj
                    if rotated:
                        eng.wait_ge(pj_done, at.jobs(u + 1))
                        eng.tensor_tensor(rb[:], pj[:], W["sin"][:], ALU.mult).then_inc(pj_free, 1)
                        eng.wait_ge(pj_free, at.jobs(u + 1))
                        eng.tensor_tensor(rot[:], ra[:], rb[:], ALU.add).then_inc(ro_done, 1)
                        src = rot
                        eng.wait_ge(ro_done, at.groups(turn, 2))
                    hi, lo = (qh, ql) if what[0] == "q" else (kh, kl)
                    eng.wait_ge(qh_done, at.groups(turn, 2))
                    ins = eng.scalar_tensor_tensor(lo[:, g % 2, :], src[:], scale_of(what), hi[:, g % 2, :].bitcast(F32),
                                                   ALU.mult, ALU.subtract)
                    ins.then_inc(ql_done if rotated else pj_free, 1)

        def pool_step(eng, s, at):
            if 0 <= s < NH:
                eng.wait_ge(rinv_done, at.heads(s + 1))
                settle(eng)
                for i in ORDER:
                    c = slice(S_AT[i], S_AT[i] + WIDTH[i])
                    last = eng.tensor_scalar(probs[:, s % 2, c], probs[:, s % 2, c], rinv[:, s % 2, i:i + 1], None, ALU.mult)
                last.then_inc(norm_done, 1)

        res_t = res_d.rearrange("(t p) d -> t p d", p=P)
        dst_t = dst_d.rearrange("(t p) d -> t p d", p=P)

        def load_xt(eng, b, at):
            for t, src in ((xth, xt_d[0]), (xtl, xt_d[1])):
                eng.dma_start(t[:, b % XB].bitcast(F32).rearrange("p k n -> p (k n)"),
                              one(src, at.batches(b), "a p n -> (a p) n")).then_inc(xt_in[b % XB], 16)

        def load_res(eng, b, t, at):
            eng.dma_start(res[:, t % 2, :], one(res_t, at.batches(RT * b + t, RT), "a p d -> (a p) d")
                          ).then_inc(res_in[t % 2], 16)

        batches = groups // per_batch

        def sp_step(eng, s, at):
            for job in jobs(s):
                what, g, t = job
                b = g // per_batch
                if what == "out":
                    eng.wait_ge(pj_free, at.jobs(number[job] + 1))
                    eng.dma_start(one(dst_t, at.batches(RT * b + t, RT), "a p d -> (a p) d"),
                                  osb[:, t % 2, :]).then_inc(stored[t % 2], 16)
                    nb, nt_ = (b, t + 2) if t < 2 else (b + 1, t - 2)
                    if nb < batches:
                        load_res(eng, nb, nt_, at)
                end_of = ("v", g, RT - 1) if per_batch == 1 else ("k", (b + 1) * per_batch - 1, 0)
                if job == end_of and b + XB < batches:
                    eng.wait_ge(pj_done, at.jobs(number[job] + 1))
                    load_xt(eng, b + XB, at)

        def sp(eng):
            for b in range(XB):
                load_xt(eng, b, At())
            for t in range(2):
                load_res(eng, 0, t, At())
            run(eng, sp_step)
            for q in range(2):
                eng.wait_ge(stored[q], 16 * 2 * batches)

        return dict(sp=sp, pool=lambda e: run(e, pool_step), act=lambda e: run(e, act_step),
                    dve=lambda e: run(e, dve_step), pe=lambda e: run(e, pe_step))

    def strips(stack, L):
        return [sb(stack, f"v_strip_{s}_{L}", [P, RT, 640], F32R) for s in ("hi", "lo")]

    def with_zero_strips(stage, pair, done):
        def pool(eng):
            for t in pair:
                last = eng.memset(t[:].bitcast(F32), 0.0)
            last.then_inc(done, 1)
            eng.wait_ge(done, 1)
        return dict(stage, pool=pool)

    stages = [prepare_stage(), norm_stage(), route_stage()]
    routing.close()

    layer0 = ExitStack()
    W0 = {}
    for name in ("qA", "qB", "kA", "kB", "v"):
        for s in ("hi", "lo"):
            W0[f"{name}_{s}"] = sb(layer0, f"w0_{name}_{s}", [P, KC, P], F32R)
            W0[f"b{name}_{s}"] = sb(layer0, f"b0_{name}_{s}", [1, P], F32R)
    for s in ("hi", "lo"):
        W0[f"o_{s}"] = sb(layer0, f"w0_o_{s}", [P, 1, D], F32R)
        W0[f"bo_{s}"] = sb(layer0, f"b0_o_{s}", [1, D], F32R)
    W0["ones_r"] = sb(layer0, "ones_r", [1, SEQ], F32R)
    W0["cos"] = sb(layer0, "cos_sb", [P, SEQ])
    W0["sin"] = sb(layer0, "sin_sb", [P, SEQ])
    strip0 = strips(layer0, "l0")
    stages.append(with_zero_strips(weights0_stage(W0), strip0, sem("strip0_zero")))
    x_rows = x.rearrange("b t d -> (b t) d")
    out_rows = out.rearrange("b t d -> (b t) d")
    stages.append(attention_stage("l0", W0, strip0, BATCH, 2, 1, True, xt0_d, x_rows, r0_d))
    layer0.close()

    stages.append(expert_stage())
    stages.append(mlp_stage())
    ternary.close()

    layer1 = ExitStack()
    W1 = {s: sb(layer1, f"w1_{s}", [P, KC, 4 * D], F32R) for s in ("hi", "lo")}
    for n, name in enumerate(("q", "k", "v", "o")):
        for s in ("hi", "lo"):
            W1[f"{name}_{s}"] = W1[s][:, :, n * D:(n + 1) * D]
    strip1 = strips(layer1, "l1")
    stages.append(with_zero_strips(weights1_stage(W1), strip1, sem("strip1_zero")))
    stages.append(attention_stage("l1", W1, strip1, BATCH * 4, 4, 4, False, xt1_d, r1_d, out_rows))
    layer1.close()

    block = ctx.enter_context(nc.Block())

    def program(eng, name):
        for k, stage in enumerate(stages):
            begin(eng, k)
            stage[name](eng)
            if k + 1 < len(stages):
                end(eng)

    @block.sync
    def _(sp):
        program(sp, "sp")

    @block.gpsimd
    def _(pool):
        program(pool, "pool")

    @block.scalar
    def _(act):
        program(act, "act")

    @block.vector
    def _(dve):
        program(dve, "dve")

    @block.tensor
    def _(pe):
        program(pe, "pe")

    ctx.close()


NAMES = ["L0_attn_x", "L0_attn_Wq", "L0_attn_bq", "L0_attn_Wk", "L0_attn_bk", "L0_attn_Wv", "L0_attn_bv", "L0_attn_Wo",
         "L0_attn_bo", "L0_ffn_w_gate", "L0_ffn_w1", "L0_ffn_w3", "L0_ffn_w2", "L1_attn_w_qkv", "L1_attn_w_out",
         "L1_ffn_w_fc", "L1_ffn_w_proj"]


def kernel(**inputs):
    import numpy as np
    import concourse.bacc as bacc
    from concourse.bass_utils import run_bass_kernel_spmd

    inv_freq = (np.float32(1.0) / np.float32(10000.0) ** (np.arange(HD // 2, dtype=np.float32) * np.float32(2.0) / np.float32(HD))
                ).astype(np.float32)
    angle = (np.arange(SEQ, dtype=np.float32)[None, :] * np.tile(inv_freq, P // (HD // 2))[:, None]).astype(np.float32)

    nc = bacc.Bacc("TRN2", target_bir_lowering=False, num_devices=1)
    arrays, args = {}, []
    for name in NAMES:
        a = np.ascontiguousarray(inputs[name])
        arrays[f"in_{name}"] = a
        args.append(nc.dram_tensor(f"in_{name}", a.shape, mybir.dt.from_np(a.dtype), kind="ExternalInput").ap())
    for name, a in (("cos", np.cos(angle)), ("sin", np.sin(angle))):
        arrays[f"in_{name}"] = a
        args.append(nc.dram_tensor(f"in_{name}", a.shape, F32, kind="ExternalInput").ap())
    args.append(nc.dram_tensor("out_0", (BATCH, SEQ, D), F32, kind="ExternalOutput").ap())
    build(nc, *args)
    r = run_bass_kernel_spmd(nc, [arrays], core_ids=[0])
    return r.results[0]["out_0"]
```

```python
from contextlib import ExitStack

import concourse.bass as bass
from concourse import mybir

F32 = mybir.dt.float32
F32R = mybir.dt.float32r
BF16 = mybir.dt.bfloat16
I32 = mybir.dt.int32
ACT = mybir.ActivationFunctionType
ALU = mybir.AluOpType
AX = mybir.AxisListType.X

P = 128
BATCH, SEQ, D = 4, 512, 512
TOKENS = BATCH * SEQ
KC = D // P
RT = SEQ // P
NT = TOKENS // P
HD = 32
HPG = P // HD
EXPERTS, TOPK, INNER = 8, 2, 1024
SOFTCAP = 30.0
HID = 1280
HM = HID // P
EPS = 1e-5
NEG = -1e30

SLOTS = 256
TILES = (TOPK * TOKENS + EXPERTS * (SLOTS - 1)) // SLOTS
FEWEST = -(-TOPK * TOKENS // SLOTS)
NSLOT = TILES * SLOTS
SC = NSLOT // P
CH = 4
CW = INNER // CH
CSUB = CW // P
UPW = KC * CW
CHW = 2 * UPW + CSUB * D


def chain(eng, sem, start):
    count = [0]

    def link(ins):
        count[0] += 1
        ins.then_inc(sem, 1)
        eng.wait_ge(sem, start + count[0])
    return link


def repeat(eng, n, body):
    body(0, True)
    with eng.Fori(1, n) as i:
        body(i, False)


def turns(eng, turn):
    turn(0, True, False)
    with eng.Fori(1, BATCH - 1) as i:
        turn(i, False, False)
    turn(BATCH - 1, False, True)


def one(ap, i, pattern):
    return ap[bass.ds(i, 1)].rearrange(pattern)


def build(nc, x, wq, bq, wk, bk, wv, bv, wo, bo, w_gate, w1, w3, w2, w_qkv, w_out, w_fc, w_proj, cos, sin, out):
    ctx = ExitStack()

    def dram(name, shape, dt=F32):
        return nc.dram_tensor(name, shape, dt).ap()

    xn_d = dram("xn_d", (TOKENS, D))
    xt0_d = [dram(f"xt0_{s}", (BATCH, P, KC * SEQ)) for s in ("hi", "lo")]
    xt1_d = [dram(f"xt1_{s}", (BATCH, P, KC * SEQ)) for s in ("hi", "lo")]
    r0_d = dram("r0_d", (TOKENS, D))
    r1_d = dram("r1_d", (TOKENS, D))
    slot_tok_d = dram("slot_tok_d", (NSLOT, 1))
    y_d = dram("y_d", (NSLOT, D))

    def sb(stack, name, shape, dt=F32, side="left"):
        return stack.enter_context(nc.sbuf_tensor(name, shape, dt, side=side))

    def ps(stack, name, shape, dt=F32):
        return stack.enter_context(nc.psum_tensor(name, shape, dt))

    def sem(name):
        return ctx.enter_context(nc.semaphore(name))

    stage_done = sem("stage_done")

    passed = sem("passed")

    def settle(eng):
        eng.sem_inc(passed, 1)

    def end(eng):
        eng.drain().then_inc(stage_done, 1)

    def begin(eng, k):
        if k:
            eng.wait_ge(stage_done, 5 * k)

    ident = sb(ctx, "ident", [P, P])
    ident_b = sb(ctx, "ident_b", [P, P], BF16)
    mask_b = sb(ctx, "mask_b", [P, P], BF16)
    before_b = sb(ctx, "before_b", [P, P], BF16)
    ones_b = sb(ctx, "ones_b", [P, P], BF16)
    ones = sb(ctx, "ones", [P, P])
    slot = sb(ctx, "slot", [P, TOPK, NT], I32)
    slot_w = sb(ctx, "slot_w", [P, TOPK, NT])
    tile_expert = sb(ctx, "tile_expert", [P, TILES + 1], I32)
    before_last = sb(ctx, "before_last", [P, 1], I32)
    slot_token = sb(ctx, "slot_token", [P, SC], I32)
    fc_scale = sb(ctx, "fc_scale", [P, 1])
    proj_scale = sb(ctx, "proj_scale", [P, 1])

    layer0 = ExitStack()
    W0 = {}
    for name in ("qA", "qB", "kA", "kB", "v"):
        for s in ("hi", "lo"):
            W0[f"{name}_{s}"] = sb(layer0, f"w0_{name}_{s}", [P, KC, P], F32R)
            W0[f"b{name}_{s}"] = sb(layer0, f"b0_{name}_{s}", [1, P], F32R)
    tern_sign = sb(layer0, "tern_sign", [P, 2, HM, D], BF16)
    raw_ternary = ExitStack()
    tern_raw = sb(raw_ternary, "tern_raw", [P, 2, HM, D], side="right")
    raw_ternary.close()
    ternary = ExitStack()
    projT = sb(ternary, "projT", [P, HM, D], F32R, side="right")
    fcT = sb(ternary, "fcT", [P, KC, HID], F32R, side="right")
    thr = sb(layer0, "thr", [P, 2, 2])
    token = sb(layer0, "token", [P, NT])
    tern_in = [sem(f"tern_in{m}") for m in range(2)]
    early = {}
    const_done, thr_done, sign_step = sem("const_done"), sem("thr_done"), sem("sign_step")

    def constants(eng):
        eng.memset(ident[:], 0.0).then_inc(const_done, 1)
        eng.memset(ident_b[:], 0.0).then_inc(const_done, 1)
        eng.memset(mask_b[:], 0.0).then_inc(const_done, 1)
        eng.memset(before_b[:], 0.0).then_inc(const_done, 1)
        eng.memset(ones_b[:], 1.0).then_inc(const_done, 1)
        eng.memset(ones[:], 1.0).then_inc(const_done, 1)
        eng.wait_ge(const_done, 6)
        for t, op, fill in ((ident, ALU.not_equal, 1.0), (ident_b, ALU.not_equal, 1.0),
                            (mask_b, ALU.is_ge, NEG), (before_b, ALU.is_ge, 1.0)):
            eng.affine_select(out=t[:], in_=t[:], compare_op=op, fill=fill, base=0,
                              pattern=[[-1, P]], channel_multiplier=1).then_inc(const_done, 1)

    SLABS = 8

    def ternary_signs(eng, low):
        link = chain(eng, sign_step, 0)
        width = HM * D // SLABS
        for m in range(2):
            raw_, sign = (t[:, m].rearrange("p a b -> p (a b)") for t in (tern_raw, tern_sign))
            for n in range(SLABS):
                c = slice(n * width, (n + 1) * width)
                link(eng.tensor_scalar(low[:], raw_[:, c], thr[:, m, 1:2], None, ALU.is_lt))
                link(eng.tensor_scalar(raw_[:, c], raw_[:, c], thr[:, m, 0:1], None, ALU.is_gt))
                link(eng.tensor_tensor(sign[:, c], raw_[:, c], low[:], ALU.subtract))

    def sign_block(k, c):
        m, n = divmod(k, HM)
        if m == 0:
            return tern_sign[:, 0, n, c * P:(c + 1) * P]
        flat = tern_sign[:, 1].rearrange("p a b -> p (a b)")
        return flat[:, c * HID + n * P:c * HID + (n + 1) * P]

    def sign_slice(k):
        m, n = divmod(k, HM)
        if m == 0:
            return fcT[:, :, n * P:(n + 1) * P]
        return projT[:, n, :].rearrange("p (c q) -> p c q", c=KC)

    LN_STEPS = 8

    def norm_buffers(stack, name):
        return dict(stats=sb(stack, name + "_stats", [P, RT, 6]), mv=sb(stack, name + "_mv", [P, RT, 2]),
                    var=sb(stack, name + "_var", [P, RT]), rstd=sb(stack, name + "_rstd", [P, RT]),
                    tmp=sb(stack, name + "_tmp", [P, RT]))

    def statistics(dve, src, ln, t):
        return dve.bn_stats(ln["stats"][:, t, :], src[:, t, :])

    def layer_norm(dve, ln, step, start, sqrt_done, sqrt_value, last):
        stats, mv, var, rstd, tmp = (ln[n] for n in ("stats", "mv", "var", "rstd", "tmp"))
        link = chain(dve, step, start)
        link(last)
        settle(dve)
        for t in range(RT):
            last = dve.bn_aggr(mv[:, t, :], stats[:, t, :])
        link(last)
        link(dve.tensor_scalar(var[:], mv[:, :, 1], EPS, None, ALU.add))
        dve.wait_ge(sqrt_done, sqrt_value)
        link(dve.reciprocal(rstd[:], rstd[:]))
        link(dve.tensor_tensor(tmp[:], rstd[:], rstd[:], ALU.mult))
        link(dve.tensor_tensor(tmp[:], tmp[:], var[:], ALU.mult))
        link(dve.tensor_scalar(tmp[:], tmp[:], -0.5, 1.5, ALU.mult, ALU.add))
        link(dve.tensor_tensor(rstd[:], rstd[:], tmp[:], ALU.mult))

    def normed(dve, src, dst, ln):
        for t in range(RT):
            last = dve.tensor_scalar(dst[:, t, :], src[:, t, :], ln["mv"][:, t, 0:1], ln["rstd"][:, t:t + 1],
                                     ALU.subtract, ALU.mult)
        return last

    def rows(ap):
        return ap.rearrange("(k p) n -> p k n", p=P)

    def weights0(W, strips, st):
        G = 4
        rq = sb(st, "wq_raw", [P, KC, D])
        rk = sb(st, "wk_raw", [P, KC, P])
        rv = sb(st, "wv_raw", [P, KC, P])
        rwo = sb(st, "wo_raw", [P, D])
        qsum = sb(st, "q_sum", [P, KC, P])
        braw = sb(st, "b_raw", [1, D + 2 * P])
        bor = sb(st, "bo_raw", [1, D])
        bsum = sb(st, "bq_sum", [1, P])
        w_in0, w_step = sem("w0_in"), sem("w0_step")
        strips_zero = sem("strips0_zero")

        def sp(eng):
            eng.dma_start(rq[:], rows(wq)).then_inc(w_in0, 16)
            eng.dma_start(rk[:], rows(wk)).then_inc(w_in0, 16)
            eng.dma_start(rv[:], rows(wv)).then_inc(w_in0, 16)
            eng.dma_start(rwo[:], wo).then_inc(w_in0, 16)
            row = "(o n) -> o n"
            eng.dma_start(braw[:, 0:D], bq.rearrange(row, o=1)).then_inc(w_in0, 16)
            eng.dma_start(braw[:, D:D + P], bk.rearrange(row, o=1)).then_inc(w_in0, 16)
            eng.dma_start(braw[:, D + P:], bv.rearrange(row, o=1)).then_inc(w_in0, 16)
            eng.dma_start(bor[:], bo.rearrange(row, o=1)).then_inc(w_in0, 16)
            eng.dma_start(W["cos"][:], cos).then_inc(w_in0, 16)
            eng.dma_start(W["sin"][:], sin).then_inc(w_in0, 16)

        def pool(eng):
            for t in strips:
                eng.memset(t[:].bitcast(F32), 0.0).then_inc(strips_zero, 1)
            link = chain(eng, w_step, 0)
            eng.wait_ge(w_in0, 160)
            for r, s in ((rq[:].rearrange("p k n -> p (k n)"), qsum[:].rearrange("p k n -> p (k n)")),
                         (braw[:, 0:D], bsum[:])):
                heads = r.rearrange("p (h g d) -> p h g d", g=G, d=HD)
                total = s.rearrange("p (h d) -> p h d", d=HD)
                link(eng.tensor_tensor(total, heads[:, :, 0, :], heads[:, :, 1, :], ALU.add))
                for g in (2, 3):
                    link(eng.tensor_tensor(total, total, heads[:, :, g, :], ALU.add))

            def split_turned(src, name):
                a_hi, a_lo, b_hi, b_lo = (W[f"{name}{v}_{s}"] for v in "AB" for s in ("hi", "lo"))

                def halves(t):
                    flat = t[:].rearrange("p k n -> p (k n)") if len(t.shape) == 3 else t[:]
                    return flat.rearrange("p (h two i) -> p h two i", two=2, i=HD // 2)
                pairs = src.rearrange("p (h i two) -> p h two i", two=2, i=HD // 2)
                link(eng.tensor_copy(halves(a_hi), pairs))
                link(eng.tensor_tensor(halves(a_lo), pairs, halves(a_hi).bitcast(F32), ALU.subtract))
                for a, b in ((a_hi, b_hi), (a_lo, b_lo)):
                    a, b = halves(a), halves(b)
                    link(eng.tensor_scalar(b[:, :, 0, :], a[:, :, 1, :].bitcast(F32), -1.0, None, ALU.mult))
                    link(eng.tensor_copy(b[:, :, 1, :], a[:, :, 0, :].bitcast(F32)))

            def split(src, hi, lo):
                link(eng.tensor_copy(hi, src))
                link(eng.tensor_tensor(lo, src, hi.bitcast(F32), ALU.subtract))

            split_turned(qsum[:].rearrange("p k n -> p (k n)"), "q")
            split_turned(rk[:].rearrange("p k n -> p (k n)"), "k")
            split_turned(bsum[:], "bq")
            split_turned(braw[:, D:D + P], "bk")
            split(rv[:], W["v_hi"][:], W["v_lo"][:])
            split(braw[:, D + P:], W["bv_hi"][:], W["bv_lo"][:])
            split(rwo[:], W["o_hi"][:, 0, :], W["o_lo"][:, 0, :])
            split(bor[:], W["bo_hi"][:], W["bo_lo"][:])
            link(eng.tensor_copy(W["ones_r"][:], ones[0:1, 0:1].to_broadcast([1, SEQ])))

        return dict(sp=sp, pool=pool)

    logits = sb(layer0, "logits", [P, NT, EXPERTS])

    def norm_stage(weights):
        st = ExitStack()
        xin = sb(st, "xin", [P, BATCH, RT, D])
        xn = sb(st, "xn", [P, RT, D])
        xth = sb(st, "xt_hi", [P, KC, SEQ], F32R)
        xtl = sb(st, "xt_lo", [P, KC, SEQ], F32R)
        wg = sb(st, "wg", [P, KC, EXPERTS])
        wgh = sb(st, "wg_hi", [P, KC, P], F32R)
        wgl = sb(st, "wg_lo", [P, KC, P], F32R)
        lgT = sb(st, "logitsT", [EXPERTS, SEQ])
        ln = norm_buffers(st, "ln0")
        xt_ps = ps(st, "xt_ps", [P, KC, SEQ])
        lgT_ps = ps(st, "lgT_ps", [P, SEQ])
        lg_ps = ps(st, "lg_ps", [P, RT * EXPERTS])
        attend = weights(st)
        st.close()

        x_in = [sem(f"x_in{b}") for b in range(BATCH)]
        wg_in, wg_zero, wg_split = sem("wg_in"), sem("wg_zero"), sem("wg_split")
        ln_step, sqrt_done = sem("ln0_step"), sem("ln0_sqrt_done")
        xn_ready, xn_stored = sem("xn_ready"), sem("xn_stored")
        xt_done, xth_done, xtl_done = sem("xt_done"), sem("xth_done"), sem("xtl_done")
        xt_stored = sem("xt_stored")
        lgT_done, lgT_copied = sem("lgT_done"), sem("lgT_copied")
        lg_done, lg_copied = sem("lg_done"), sem("lg_copied")

        x_b = x.rearrange("b (t p) d -> b p t d", p=P)
        xn_b = xn_d.rearrange("(b t p) d -> b p t d", b=BATCH, p=P)

        def x_of(b):
            return xin[:, bass.ds(b, 1)].rearrange("p a t d -> p (a t) d")

        def pool(eng):
            constants(eng)
            eng.iota(token[:], pattern=[[P, NT]], base=0, channel_multiplier=1,
                     allow_small_or_imprecise_dtypes=True)
            attend["pool"](eng)

        def sp(eng):
            for b in range(BATCH):
                eng.dma_start(xin[:, b], x_b[b]).then_inc(x_in[b], 16)
                if b == 0:
                    eng.dma_start(wg[:], w_gate.rearrange("(k p) e -> p k e", p=P)).then_inc(wg_in, 16)
                    attend["sp"](eng)

            def turn(b, first):
                eng.wait_ge(xn_ready, b + 1)
                eng.dma_start(one(xn_b, b, "a p t d -> (a p) t d"), xn[:]).then_inc(xn_stored, 16)
                eng.wait_ge(xtl_done, KC * b + KC)
                for s, t in enumerate((xth, xtl)):
                    eng.dma_start(one(xt0_d[s], b, "a p n -> (a p) n"),
                                  t[:].bitcast(F32).rearrange("p k n -> p (k n)")).then_inc(xt_stored, 16)
            repeat(eng, BATCH, turn)
            eng.dma_start(tern_raw[:, 0], w_fc.rearrange("(n p) d -> p n d", p=P)).then_inc(tern_in[0], 16)
            eng.dma_start(tern_raw[:, 1].rearrange("p a b -> p (a b)").rearrange("p (n h) -> p n h", n=KC),
                          w_proj.rearrange("(n p) h -> p n h", p=P)).then_inc(tern_in[1], 16)
            eng.wait_ge(xn_stored, 16 * BATCH)
            eng.wait_ge(xt_stored, 32 * BATCH)

        def act(eng):
            def root(b):
                eng.wait_ge(ln_step, LN_STEPS * b + 3)
                nc.scalar.activation(ln["rstd"][:], ln["var"][:], ACT.Sqrt).then_inc(sqrt_done, 1)

            def turn(b, first, last):
                if not last:
                    root(b + 1)
                if not first:
                    eng.wait_ge(xt_stored, 32 * b)
                    eng.wait_ge(lgT_done, b)
                for k in range(KC):
                    eng.wait_ge(xt_done, KC * b + k + 1)
                    nc.scalar.copy(xth[:, k, :], xt_ps[:, k, :]).then_inc(xth_done, 1)
                eng.wait_ge(lgT_done, b + 1)
                if not first:
                    eng.wait_ge(lg_done, b)
                nc.scalar.copy(lgT[:], lgT_ps[0:EXPERTS, :]).then_inc(lgT_copied, 1)
                eng.wait_ge(lg_done, b + 1)
                nc.scalar.copy(logits[:].rearrange("p t e -> p (t e)")[:, bass.ds(b * (RT * EXPERTS), RT * EXPERTS)],
                               lg_ps[:]).then_inc(lg_copied, 1)
            root(0)
            turns(eng, turn)

        def dve(eng):
            def turn(b, first, last):
                if first:
                    eng.wait_ge(x_in[1], 16)
                if not last:
                    stats(b + 1)
                if not first:
                    eng.wait_ge(xt_stored, 32 * b)
                    eng.wait_ge(lgT_done, b)
                for k in range(KC):
                    eng.wait_ge(xth_done, KC * b + k + 1)
                    eng.tensor_tensor(xtl[:, k, :], xt_ps[:, k, :], xth[:, k, :].bitcast(F32),
                                      ALU.subtract).then_inc(xtl_done, 1)
                if not last:
                    eng.wait_ge(xt_done, KC * (b + 1))
                    eng.wait_ge(xn_stored, 16 * (b + 1))
                    normed(eng, x_of(b + 1), xn, ln).then_inc(xn_ready, 1)
                if first:
                    for later in range(2, BATCH):
                        eng.wait_ge(x_in[later], 16)

            def stats(b):
                for t in range(RT):
                    last = statistics(eng, x_of(b), ln, t)
                layer_norm(eng, ln, ln_step, LN_STEPS * b, sqrt_done, b + 1, last)

            eng.memset(wgh[:].bitcast(F32), 0.0)
            eng.memset(wgl[:].bitcast(F32), 0.0).then_inc(wg_zero, 1)
            eng.wait_ge(x_in[0], 16)
            stats(0)
            normed(eng, x_of(0), xn, ln).then_inc(xn_ready, 1)
            eng.wait_ge(wg_zero, 1)
            eng.wait_ge(wg_in, 16)
            eng.tensor_copy(wgh[:, :, 0:EXPERTS], wg[:]).then_inc(wg_split, 1)
            eng.wait_ge(wg_split, 1)
            eng.tensor_tensor(wgl[:, :, 0:EXPERTS], wg[:], wgh[:, :, 0:EXPERTS].bitcast(F32),
                              ALU.subtract).then_inc(wg_split, 1)
            turns(eng, turn)

        def pe(eng):
            eng.wait_ge(const_done, 10)

            def turn(b, first, last):
                eng.wait_ge(xn_ready, b + 1)
                for k in range(KC):
                    if not first:
                        eng.wait_ge(xtl_done, KC * (b - 1) + k + 1)
                    for t in range(RT):
                        end_ = eng.transpose(xt_ps[:, k, t * P:(t + 1) * P], xn[:, t, k * P:(k + 1) * P], ident[:])
                    end_.then_inc(xt_done, 1)
                if first:
                    eng.wait_ge(wg_split, 2)
                else:
                    eng.wait_ge(lgT_copied, b)
                for k in range(KC):
                    eng.wait_ge(xtl_done, KC * b + k + 1)
                    for w, v in ((wgh, xth), (wgh, xtl), (wgl, xth)):
                        end_ = eng.matmul(lgT_ps[:], w[:, k, :], v[:, k, :], start=(k == 0 and w is wgh and v is xth),
                                          stop=(k == KC - 1 and w is wgl))
                end_.then_inc(lgT_done, 1)
                eng.wait_ge(lgT_copied, b + 1)
                if not first:
                    eng.wait_ge(lg_copied, b)
                    settle(eng)
                for t in range(RT):
                    end_ = eng.transpose(lg_ps[:, t * EXPERTS:(t + 1) * EXPERTS], lgT[:, t * P:(t + 1) * P],
                                         ident[0:EXPERTS, 0:EXPERTS])
                end_.then_inc(lg_done, 1)
            turns(eng, turn)

        return dict(sp=sp, pool=pool, act=act, dve=dve, pe=pe)

    def route_stage():
        st = ExitStack()
        shape = [P, NT, EXPERTS]
        probs = sb(st, "probs", shape)
        picked = [sb(st, f"picked{k}", shape) for k in range(TOPK)]
        work = sb(st, "work", shape)
        e_iota = sb(st, "e_iota", shape)
        e_below = sb(st, "e_below", shape)
        row = sb(st, "row", [P, NT])
        chosen = sb(st, "chosen", shape, BF16)
        ahead = sb(st, "ahead", [P, NT + 1, EXPERTS], BF16)
        steps = sb(st, "steps", [P, EXPERTS, EXPERTS])
        tile_i = sb(st, "tile_i", [P, TILES + 1, EXPERTS])
        tile_w = sb(st, "tile_w", [P, TILES + 1, EXPERTS])
        tile_f = sb(st, "tile_f", [P, TILES + 1])
        ntile = sb(st, "ntile", [P, EXPERTS])
        upto = sb(st, "upto", [P, EXPERTS])
        base = sb(st, "base", [P, EXPERTS])
        sums = sb(st, "abs_sums", [P, 2, HM])
        magnitude = sb(st, "abs_values", [P, 2, D])
        tot = sb(st, "abs_tot", [P, 2])
        mean = sb(st, "abs_mean", [P, 2])
        slot_f = sb(st, "slot_f", [P, TOPK, NT])
        rank_ps = ps(st, "rank_ps", [P, NT * EXPERTS])
        count_ps = ps(st, "count_ps", [P, EXPERTS])
        tot_ps = ps(st, "tot_ps", [P, 2])
        st.close()
        iota_done, abs_done, tot_done, sum_done = sem("iota_done"), sem("abs_done"), sem("abs_tot_done"), sem("abs_sum_done")
        tanh_ready, tanh_done, exp_ready, exp_done0 = (sem(n) for n in ("tanh_ready", "tanh_done", "exp_ready", "exp_done0"))
        r_step, ahead_done, rank_done = sem("r_step"), sem("ahead_done"), sem("rank_done")
        slot_done = sem("slot_done")

        def pool(eng):
            eng.iota(e_iota[:], pattern=[[0, NT], [1, EXPERTS]], base=0, channel_multiplier=0,
                     allow_small_or_imprecise_dtypes=True)
            eng.iota(e_below[:], pattern=[[0, NT], [1, EXPERTS]], base=-EXPERTS, channel_multiplier=0,
                     allow_small_or_imprecise_dtypes=True)
            eng.iota(steps[:], pattern=[[0, EXPERTS], [SLOTS, EXPERTS]], base=0, channel_multiplier=0,
                     allow_small_or_imprecise_dtypes=True)
            eng.iota(tile_i[:], pattern=[[1, TILES + 1], [0, EXPERTS]], base=0, channel_multiplier=0,
                     allow_small_or_imprecise_dtypes=True).then_inc(iota_done, 1)

        def act(eng):
            nc.scalar.activation(probs[:], logits[:], ACT.Tanh, scale=1.0 / SOFTCAP).then_inc(tanh_done, 1)
            eng.wait_ge(exp_ready, 1)
            nc.scalar.activation(probs[:], work[:], ACT.Exp, scale=SOFTCAP).then_inc(exp_done0, 1)
            for m in range(2):
                eng.wait_ge(tern_in[m], 16)
                for n in range(HM):
                    nc.scalar.activation(magnitude[:, n % 2], tern_raw[:, m, n], ACT.Abs,
                                         accum_out=sums[:, m, n:n + 1]).then_inc(abs_done, 1)
                    if HM * m + n:
                        eng.wait_ge(abs_done, HM * m + n)

        def pe(eng):
            eng.wait_ge(ahead_done, 1)
            flat = ahead[:].rearrange("p t e -> p (t e)")
            eng.matmul(rank_ps[:], before_b[:], chosen[:].rearrange("p t e -> p (t e)"), start=True, stop=False)
            eng.matmul(rank_ps[:], ones_b[:], flat[:, 0:NT * EXPERTS], start=False, stop=True)
            eng.matmul(count_ps[:], ones_b[:], flat[:, NT * EXPERTS:], start=True, stop=True).then_inc(rank_done, 1)
            eng.wait_ge(tot_done, 1)
            eng.matmul(tot_ps[:], ones[:], tot[:], start=True, stop=True).then_inc(sum_done, 1)

        def dve(eng):
            link = chain(eng, r_step, 0)

            def over_e(ap):
                return ap.unsqueeze(2).to_broadcast(shape)

            eng.wait_ge(tanh_done, 1)
            link(eng.tensor_reduce(row[:], probs[:], AX, ALU.max))
            eng.tensor_tensor(work[:], probs[:], over_e(row[:]), ALU.subtract).then_inc(exp_ready, 1)
            eng.wait_ge(exp_done0, 1)
            link(eng.tensor_reduce(row[:], probs[:], AX, ALU.add))
            link(eng.reciprocal(row[:], row[:]))
            link(eng.tensor_tensor(probs[:], probs[:], over_e(row[:]), ALU.mult))
            eng.wait_ge(iota_done, 1)
            for k in range(TOPK):
                link(eng.tensor_reduce(slot_w[:, k, :], probs[:], AX, ALU.max))
                link(eng.tensor_tensor(work[:], probs[:], over_e(slot_w[:, k, :]), ALU.is_equal))
                link(eng.scalar_tensor_tensor(work[:], work[:], -float(EXPERTS), e_iota[:], ALU.mult, ALU.add))
                link(eng.tensor_reduce(row[:], work[:], AX, ALU.min))
                link(eng.tensor_tensor(picked[k][:], e_below[:], over_e(row[:]), ALU.is_equal))
                if k == 0:
                    link(eng.scalar_tensor_tensor(probs[:], picked[0][:], -2.0, probs[:], ALU.mult, ALU.add))
            link(eng.tensor_tensor(chosen[:], picked[0][:], picked[1][:], ALU.add))
            link(eng.memset(ahead[:, 0, :], 0.0))
            for t in range(NT):
                link(eng.tensor_tensor(ahead[:, t + 1, :], ahead[:, t, :], chosen[:, t, :], ALU.add))
            eng.nop().then_inc(ahead_done, 1)
            eng.wait_ge(rank_done, 1)
            e2 = [P, EXPERTS, EXPERTS]
            link(eng.tensor_copy(ntile[:], count_ps[:]))
            link(eng.tensor_tensor(steps[:], ntile[:].unsqueeze(2).to_broadcast(e2), steps[:], ALU.is_gt))
            link(eng.tensor_reduce(ntile[:], steps[:], AX, ALU.add))
            link(eng.tensor_copy(upto[:, 0:1], ntile[:, 0:1]))
            for e in range(1, EXPERTS):
                link(eng.tensor_tensor(upto[:, e:e + 1], upto[:, e - 1:e], ntile[:, e:e + 1], ALU.add))
            link(eng.tensor_tensor(base[:], upto[:], ntile[:], ALU.subtract))
            link(eng.tensor_scalar(base[:], base[:], float(SLOTS), None, ALU.mult))
            link(eng.tensor_tensor(work[:], rank_ps[:].rearrange("p (t e) -> p t e", e=EXPERTS),
                                   base[:].unsqueeze(1).to_broadcast(shape), ALU.add))
            for k in range(TOPK):
                link(eng.tensor_tensor(picked[k][:], picked[k][:], work[:], ALU.mult))
                link(eng.tensor_reduce(slot_f[:, k, :], picked[k][:], AX, ALU.add))
            eng.tensor_copy(slot[:], slot_f[:]).then_inc(slot_done, 1)
            ts = [P, TILES + 1, EXPERTS]
            link(eng.tensor_tensor(tile_w[:], tile_i[:], upto[:].unsqueeze(1).to_broadcast(ts), ALU.is_ge))
            link(eng.tensor_reduce(tile_f[:], tile_w[:], AX, ALU.add))
            link(eng.tensor_scalar(tile_f[:], tile_f[:], float(EXPERTS - 1), None, ALU.min))
            eng.tensor_copy(tile_expert[:], tile_f[:])
            link(eng.tensor_scalar(ntile[:, 0:1], upto[:, EXPERTS - 1:], -2.0, None, ALU.add))
            eng.tensor_copy(before_last[:], ntile[:, 0:1])
            eng.wait_ge(abs_done, 2 * HM)
            eng.tensor_reduce(tot[:], sums[:], AX, ALU.add).then_inc(tot_done, 1)
            eng.wait_ge(sum_done, 1)
            eng.tensor_scalar(mean[:], tot_ps[:], 1.0 / (HID * D), 1e-5, ALU.mult, ALU.max).then_inc(thr_done, 1)
            eng.wait_ge(thr_done, 1)
            eng.tensor_copy(fc_scale[:], mean[:, 0:1])
            eng.tensor_copy(proj_scale[:], mean[:, 1:2])
            eng.tensor_scalar(thr[:, :, 0], mean[:], 0.7, None, ALU.mult).then_inc(thr_done, 1)
            eng.tensor_scalar(thr[:, :, 1], mean[:], -0.7, None, ALU.mult).then_inc(thr_done, 1)

        return dict(sp=lambda eng: early["xtl0"](eng), pool=pool, act=act, dve=dve, pe=pe)

    def expert_stage():
        st = ExitStack()
        raw = sb(st, "w_raw", [P, 2, CHW])
        whi = sb(st, "w_hi", [P, CH, CHW], F32R)
        wlo = sb(st, "w_lo", [P, CH, CHW], F32R)
        xg = sb(st, "x_rows", [P, 2, D])
        xidx = sb(st, "x_idx", [P, 2], I32)
        xth = sb(st, "xs_hi", [P, KC, SLOTS], F32R)
        xtl = sb(st, "xs_lo", [P, KC, SLOTS], F32R)
        sg = sb(st, "silu", [P, 2, CSUB * SLOTS])
        hh = sb(st, "h", [P, 2, CSUB * SLOTS])
        hhi = sb(st, "h_hi", [P, 2, CSUB * SLOTS], F32R)
        hlo = sb(st, "h_lo", [P, 2, CSUB * SLOTS], F32R)
        ysb = sb(st, "y_rows", [P, 2, D])
        up_ps = [[ps(st, f"up{w}_{q}", [P, CSUB * SLOTS]) for w in (1, 3)] for q in range(2)]
        y_ps = ps(st, "y_ps", [P, 2, D])
        x_ps = ps(st, "x_ps", [P, KC, SLOTS])
        st.close()
        w_in = [sem(f"w_in{r}") for r in range(2)]
        whi_done, wlo_done = sem("whi_done"), sem("wlo_done")
        idx_done, x_in, xs_t, xsh_done, xsl_done = (sem(n) for n in ("xidx_done", "xrows_in", "xs_t", "xsh_done", "xsl_done"))
        up_done, silu_done, gated, h_hi_done, h_done = (sem(n) for n in ("up_done", "silu_done", "gated", "h_hi_done", "h_done"))
        used, y_copied, y_stored = (sem(n) for n in ("chunk_used", "y_copied", "y_stored"))

        def last_of(eng):
            return eng.value_load(before_last[0:1, 0:1], min_val=FEWEST - 2, max_val=TILES - 2) + 1

        def between(eng, end_, turn):
            with eng.Fori(1, TILES) as i:
                with eng.If(i < end_):
                    turn(i)

        w1_c = w1.rearrange("e (k p) i -> e p k i", p=P)
        w3_c = w3.rearrange("e (k p) i -> e p k i", p=P)
        w2_c = w2.rearrange("e (c s p) d -> e c p s d", c=CH, p=P)
        y_t = y_d.rearrange("(i h p) d -> i p h d", h=2, p=P)

        def load(eng, e, c):
            r = c % 2
            for n, w in enumerate((w1_c, w3_c)):
                eng.dma_start(raw[:, r, n * UPW:(n + 1) * UPW].rearrange("p (k j) -> p k j", k=KC),
                              one(w, e, "a p k i -> (a p) k i")[:, :, c * CW:(c + 1) * CW]).then_inc(w_in[r], 16)
            eng.dma_start(raw[:, r, 2 * UPW:CHW].rearrange("p (s d) -> p s d", s=CSUB),
                          one(w2_c, e, "a c p s d -> (a c) p s d")[c]).then_inc(w_in[r], 16)

        def first_chunks(eng):
            e = eng.value_load(tile_expert[0:1, 0:1], min_val=0, max_val=EXPERTS - 1)
            for c in range(2):
                load(eng, e, c)
        early["experts"] = first_chunks

        def sp(eng):
            last = last_of(eng)

            def turn(i, first):
                e = eng.value_load(tile_expert[0:1, bass.ds(i, 1)], min_val=0, max_val=EXPERTS - 1)
                for c in range(CH):
                    if first and c < 2:
                        continue
                    eng.wait_ge(wlo_done, CH * i + c - 1)
                    load(eng, e, c)
            turn(0, True)
            between(eng, last + 1, lambda i: turn(i, False))

        def pool(eng):
            last = last_of(eng)

            def turn(i, first):
                if not first:
                    eng.wait_ge(xs_t, i)
                eng.tensor_copy(xidx[:], slot_token[:, bass.ds(2 * i, 2)]).then_inc(idx_done, 1)
                eng.wait_ge(idx_done, i + 1)
                settle(eng)
                for h in range(2):
                    eng.indirect_dma_start(out=xg[:, h, :], out_offset=None, in_=xn_d,
                                           in_offset=bass.IndirectOffsetOnAxis(ap=xidx[:, h:h + 1], axis=0)
                                           ).then_inc(x_in, 16)
                eng.wait_ge(x_in, 32 * i + 32)
            turn(0, True)
            between(eng, last + 1, lambda i: turn(i, False))

        def act(eng):
            def split(i, c):
                g, s, r = CH * i + c, c % CH, c % 2
                eng.wait_ge(w_in[r], 48 * (2 * i + c // 2 + 1))
                if not (isinstance(g, int) and g < CH):
                    eng.wait_ge(used, g - CH + 1)
                nc.scalar.copy(whi[:, s, :], raw[:, r, :]).then_inc(whi_done, 1)

            def xs_hi(i):
                eng.wait_ge(xs_t, i + 1)
                nc.scalar.copy(xth[:], x_ps[:]).then_inc(xsh_done, 1)

            def turn(i, first, last=False):
                for c in range(CH):
                    g = CH * i + c
                    if c == CH - 1 and not last:
                        xs_hi(i + 1)
                    eng.wait_ge(up_done, g + 1)
                    if not (first and c < 2):
                        eng.wait_ge(gated, g - 1)
                    nc.scalar.activation(sg[:, c % 2, :], up_ps[c % 2][0][:], ACT.Silu).then_inc(silu_done, 1)
                    if c == 0 and not first:
                        y_rows(i - 1, first=False)
                    if not (last and c >= 2):
                        split(i, c + 2)

            def y_rows(i, first):
                eng.wait_ge(used, CH * i + CH)
                nc.scalar.copy(ysb[:], y_ps[:]).then_inc(y_copied, 1)
                eng.wait_ge(y_copied, i + 1)
                eng.dma_start(one(y_t, i, "a p h d -> (a p) h d"), ysb[:]).then_inc(y_stored, 16)

            split(0, 0)
            split(0, 1)
            xs_hi(0)
            turn(0, True)

            def middle(i):
                turn(i, False)
                eng.wait_ge(y_stored, 16 * i)
                settle(eng)
            last = last_of(eng)
            between(eng, last, middle)
            turn(last, False, last=True)
            eng.wait_ge(y_stored, 16 * last)
            y_rows(last, first=False)
            eng.wait_ge(y_stored, 16 * last + 16)
            settle(eng)

        def dve(eng):
            def split(i, c):
                g, s, r = CH * i + c, c % CH, c % 2
                eng.wait_ge(whi_done, g + 1)
                eng.tensor_tensor(wlo[:, s, :], raw[:, r, :], whi[:, s, :].bitcast(F32), ALU.subtract).then_inc(wlo_done, 1)

            def xs_lo(i):
                eng.wait_ge(xsh_done, i + 1)
                eng.tensor_tensor(xtl[:], x_ps[:], xth[:].bitcast(F32), ALU.subtract).then_inc(xsl_done, 1)

            def turn(i, first, last=False):
                for c in range(CH):
                    g = CH * i + c
                    if c == CH - 1 and not last:
                        xs_lo(i + 1)
                    eng.wait_ge(silu_done, g + 1)
                    if not (first and c < 2):
                        eng.wait_ge(h_done, g - 1)
                    eng.tensor_tensor(hh[:, c % 2, :], sg[:, c % 2, :], up_ps[c % 2][1][:], ALU.mult).then_inc(gated, 1)
                    eng.wait_ge(gated, g + 1)
                    if not (first and c < 2):
                        eng.wait_ge(used, g - 1)
                    eng.tensor_copy(hhi[:, c % 2, :], hh[:, c % 2, :]).then_inc(h_hi_done, 1)
                    eng.wait_ge(h_hi_done, g + 1)
                    eng.tensor_tensor(hlo[:, c % 2, :], hh[:, c % 2, :], hhi[:, c % 2, :].bitcast(F32), ALU.subtract).then_inc(h_done, 1)
                    if not (last and c >= 2):
                        split(i, c + 2)
            split(0, 0)
            split(0, 1)
            xs_lo(0)
            turn(0, True)
            last = last_of(eng)
            between(eng, last, lambda i: turn(i, False))
            turn(last, False, last=True)

        def pe(eng):
            def rows_t(i, first):
                eng.wait_ge(x_in, 32 * i + 32)
                if not first:
                    eng.wait_ge(xsl_done, i)
                for k in range(KC):
                    for h in range(2):
                        last = eng.transpose(x_ps[:, k, h * P:(h + 1) * P], xg[:, h, k * P:(k + 1) * P], ident[:])
                last.then_inc(xs_t, 1)

            def up(i, c, first):
                g, s, q = CH * i + c, c % CH, c % 2
                eng.wait_ge(wlo_done, g + 1)
                if c == 0:
                    eng.wait_ge(xsl_done, i + 1)
                if not (first and c < 2):
                    eng.wait_ge(gated, g - 1)
                for n in range(2):
                    for j in range(CSUB):
                        step = 0
                        for k in range(KC):
                            at = slice(n * UPW + k * CW + j * P, n * UPW + k * CW + (j + 1) * P)
                            for w, v in ((whi, xth), (whi, xtl), (wlo, xth)):
                                last = eng.matmul(up_ps[q][n][:, j * SLOTS:(j + 1) * SLOTS], w[:, s, at], v[:, k, :],
                                                  start=(step == 0), stop=(step == 3 * KC - 1))
                                step += 1
                last.then_inc(up_done, 1)

            def down(i, c, first):
                g, q = CH * i + c, c % 2
                eng.wait_ge(h_done, g + 1)
                if c == 0 and not first:
                    eng.wait_ge(y_copied, i)
                for h in range(2):
                    step = 0
                    for j in range(CSUB):
                        at = slice(j * SLOTS + h * P, j * SLOTS + (h + 1) * P)
                        wat = slice(2 * UPW + j * D, 2 * UPW + (j + 1) * D)
                        for v, w in ((hhi, whi), (hhi, wlo), (hlo, whi)):
                            last = eng.matmul(y_ps[:, h, :], v[:, q, at], w[:, c, wat],
                                              start=(c == 0 and step == 0), stop=(c == CH - 1 and step == 3 * CSUB - 1))
                            step += 1
                last.then_inc(used, 1)

            def turn(i, first, last=False):
                up(i, 1, first)
                down(i, 0, first)
                up(i, 2, first)
                down(i, 1, first)
                up(i, 3, first)
                if not last:
                    rows_t(i + 1, False)
                down(i, 2, first)
                if not last:
                    up(i + 1, 0, False)
                down(i, 3, first)

            rows_t(0, True)
            up(0, 0, True)
            turn(0, True)
            last = last_of(eng)
            between(eng, last, lambda i: turn(i, False))
            turn(last, False, last=True)

        return dict(sp=sp, pool=pool, act=act, dve=dve, pe=pe)

    def mlp_stage(W):
        st = ExitStack()
        yg = sb(st, "y_gathered", [P, TOPK, RT, D])
        xn = yg[:, 0]
        WH = 2 * D
        raw = sb(st, "w_attn_raw", [P, 2, WH])
        x1 = sb(st, "x1", [P, BATCH, RT, D])
        yidx = sb(st, "y_idx", [P, TOPK, RT], I32)
        yw = sb(st, "y_w", [P, TOPK, RT])
        ln = norm_buffers(st, "ln1")
        xth = sb(st, "x1t_hi", [P, KC, SEQ], F32R)
        xtl = sb(st, "x1t_lo", [P, KC, SEQ], F32R)
        relu = sb(st, "relu", [P, 2, SEQ])
        sq = sb(st, "relu2", [P, 2, SEQ])
        hhi = sb(st, "relu2_hi", [P, 2, SEQ], F32R)
        hlo = sb(st, "relu2_lo", [P, 2, SEQ], F32R)
        xt_ps = [ps(st, f"x1t_ps{i}", [P, SEQ]) for i in range(2)]
        h_ps = [ps(st, f"hid_ps{i}", [P, SEQ]) for i in range(2)]
        y_ps = ps(st, "mlp_ps", [P, RT, D])
        st.close()
        r0_in = sem("r0_in")
        idx_done = sem("yidx_done")
        yg_in = [sem(f"yg_in{t}") for t in range(RT)]
        yw_done, mixed = sem("yw_done"), sem("mixed")
        ln_step, sqrt_done, xn_ready = sem("ln1_step"), sem("ln1_sqrt_done"), sem("x1n_ready")
        xt_done, xth_done, xtl_done, xt_stored = (sem(n) for n in ("x1t_done", "x1th_done", "x1tl_done", "x1t_stored"))
        hid_done, relu_done, sq_done, hhi_done, hlo_done = (
            sem(n) for n in ("hid_done", "relu_done", "sq_done", "hhi_done", "hlo_done"))
        mlp_used, res_done, res_stored = sem("mlp_used"), sem("res_done"), sem("res_stored")
        w_in1 = [sem(f"w_attn_in{h}") for h in range(2)]
        whi_done, wlo_done = sem("w_attn_hi"), sem("w_attn_lo")

        r0_b = r0_d.rearrange("(b t p) d -> b p t d", b=BATCH, p=P)
        r1_b = r1_d.rearrange("(b t p) d -> b p t d", b=BATCH, p=P)
        qkv_k, out_k = w_qkv.rearrange("(k p) n -> k p n", p=P), w_out.rearrange("(k p) n -> k p n", p=P)

        def x1_of(b):
            return x1[:, bass.ds(b, 1)].rearrange("p a t d -> p (a t) d")

        def w_half(t, b, h):
            return t[:, bass.ds(b, 1), h * WH:(h + 1) * WH].rearrange("p k n -> p (k n)")

        def sp(eng):
            def load_x(b):
                eng.dma_start(x1_of(b), one(r0_b, b, "a p t d -> (a p) t d")).then_inc(r0_in, 16)

            def load_w(b):
                eng.dma_start(raw[:, 0, :], one(qkv_k, b, "a p n -> (a p) n")[:, 0:WH]).then_inc(w_in1[0], 16)
                eng.dma_start(raw[:, 1, 0:D], one(qkv_k, b, "a p n -> (a p) n")[:, WH:]).then_inc(w_in1[1], 16)
                eng.dma_start(raw[:, 1, D:], one(out_k, b, "a p n -> (a p) n")).then_inc(w_in1[1], 16)

            def store_xt(b):
                eng.wait_ge(xtl_done, KC * b + KC)
                for s, t in enumerate((xth, xtl)):
                    eng.dma_start(one(xt1_d[s], b, "a p n -> (a p) n"),
                                  t[:].bitcast(F32).rearrange("p k n -> p (k n)")).then_inc(xt_stored, 16)

            def turn(b, first, last):
                if not last:
                    load_x(b + 1)
                    eng.wait_ge(wlo_done, 2 * b + 2)
                    load_w(b + 1)
                    store_xt(b + 1)
                else:
                    eng.wait_ge(xt_done, KC * BATCH)
                    eng.wait_ge(wlo_done, 2 * BATCH)
                    eng.wait_ge(res_stored, 16 * (BATCH - 1))
                    eng.wait_ge(xt_stored, 32 * BATCH)
                    early["xtl1"](eng)
                eng.wait_ge(res_done, b + 1)
                eng.dma_start(one(r1_b, b, "a p t d -> (a p) t d"), x1_of(b)).then_inc(res_stored, 16)
            load_x(0)
            for t in range(RT):
                eng.wait_ge(yg_in[t], 16 * TOPK)
            load_w(0)
            store_xt(0)
            turns(eng, turn)
            eng.wait_ge(xt_stored, 32 * BATCH)
            eng.wait_ge(res_stored, 16 * BATCH)

        def pool(eng):
            def gather(b):
                eng.tensor_copy(yidx[:], slot[:, :, bass.ds(RT * b, RT)]).then_inc(idx_done, 1)
                eng.wait_ge(idx_done, b + 1)
                if not (isinstance(b, int) and b == 0):
                    eng.wait_ge(xt_done, KC * b)
                    eng.wait_ge(mixed, TOPK * RT * b)
                    settle(eng)
                for t in range(RT):
                    for k in range(TOPK):
                        eng.indirect_dma_start(out=yg[:, k, t, :], out_offset=None, in_=y_d,
                                               in_offset=bass.IndirectOffsetOnAxis(ap=yidx[:, k, t:t + 1], axis=0)
                                               ).then_inc(yg_in[t], 16)

            def gathered(b):
                for t in range(RT):
                    eng.wait_ge(yg_in[t], 16 * TOPK * (b + 1))

            def turn(b, first, last):
                if not last:
                    gather(b + 1)
                    gathered(b + 1)
                    settle(eng)
            gather(0)
            gathered(0)
            turns(eng, turn)

        def act(eng):
            def root(b):
                eng.wait_ge(ln_step, LN_STEPS * b + 3)
                nc.scalar.activation(ln["rstd"][:], ln["var"][:], ACT.Sqrt).then_inc(sqrt_done, 1)

            def xt_hi(b, first=False):
                if not first:
                    eng.wait_ge(xt_stored, 32 * b)
                    eng.wait_ge(hid_done, HM * b)
                for k in range(KC):
                    eng.wait_ge(xt_done, KC * b + k + 1)
                    nc.scalar.copy(xth[:, k, :], xt_ps[k % 2][:]).then_inc(xth_done, 1)

            def turn(b, first, last):
                for m in range(HM):
                    q, g = m % 2, HM * b + m
                    eng.wait_ge(hid_done, g + 1)
                    if not (first and m < 2):
                        eng.wait_ge(mlp_used, g - 1)
                    nc.scalar.activation(relu[:, q, :], h_ps[q][:], ACT.Relu, scale=fc_scale[:, 0:1]).then_inc(relu_done, 1)
                    eng.wait_ge(relu_done, g + 1)
                    nc.scalar.activation(hhi[:, q, :], relu[:, q, :], ACT.Square).then_inc(hhi_done, 1)
                    nc.scalar.activation(sq[:, q, :], relu[:, q, :], ACT.Square).then_inc(sq_done, 1)
                    if m < 2:
                        h = m
                        eng.wait_ge(w_in1[h], 16 * (h + 1) * (b + 1))
                        nc.scalar.copy(w_half(W["hi"], b, h), raw[:, h, :]).then_inc(whi_done, 1)
                    if m == 6 and not last:
                        root(b + 1)
                if not last:
                    xt_hi(b + 1)
            root(0)
            xt_hi(0, True)
            turns(eng, turn)

        def dve(eng):
            def combine(b, t):
                if t == 0:
                    eng.tensor_copy(yw[:], slot_w[:, :, bass.ds(RT * b, RT)]).then_inc(yw_done, 1)
                    eng.wait_ge(yw_done, b + 1)
                    eng.wait_ge(r0_in, 16 * b + 16)
                eng.wait_ge(yg_in[t], 16 * TOPK * (b + 1))
                for k in range(TOPK):
                    eng.scalar_tensor_tensor(x1_of(b)[:, t, :], yg[:, k, t, :], yw[:, k, t:t + 1], x1_of(b)[:, t, :],
                                             ALU.mult, ALU.add).then_inc(mixed, 1)
                    eng.wait_ge(mixed, TOPK * (RT * b + t) + k + 1)
                settle(eng)
                return statistics(eng, x1_of(b), ln, t)

            def moments(b, last):
                layer_norm(eng, ln, ln_step, LN_STEPS * b, sqrt_done, b + 1, last)

            def xt_lo(b, first=False):
                if not first:
                    eng.wait_ge(xt_stored, 32 * b)
                    eng.wait_ge(hid_done, HM * b)
                for k in range(KC):
                    eng.wait_ge(xth_done, KC * b + k + 1)
                    eng.tensor_tensor(xtl[:, k, :], xt_ps[k % 2][:], xth[:, k, :].bitcast(F32),
                                      ALU.subtract).then_inc(xtl_done, 1)

            def turn(b, first, last):
                for m in range(HM):
                    q, g = m % 2, HM * b + m
                    eng.wait_ge(sq_done, g + 1)
                    if not (first and m < 2):
                        eng.wait_ge(mlp_used, g - 1)
                    eng.tensor_tensor(hlo[:, q, :], sq[:, q, :], hhi[:, q, :].bitcast(F32), ALU.subtract).then_inc(hlo_done, 1)
                    if m < 2:
                        h = m
                        eng.wait_ge(whi_done, 2 * b + h + 1)
                        eng.tensor_tensor(w_half(W["lo"], b, h), raw[:, h, :], w_half(W["hi"], b, h).bitcast(F32),
                                          ALU.subtract).then_inc(wlo_done, 1)
                    if last:
                        continue
                    if 3 <= m < 3 + RT:
                        end_ = combine(b + 1, m - 3)
                        if m == 2 + RT:
                            moments(b + 1, end_)
                    elif m == 3 + RT:
                        normed(eng, x1_of(b + 1), xn, ln).then_inc(xn_ready, 1)
                if not last:
                    xt_lo(b + 1)
                eng.wait_ge(mlp_used, HM * b + HM)
                for t in range(RT):
                    end_ = eng.scalar_tensor_tensor(x1_of(b)[:, t, :], y_ps[:, t, :], proj_scale[:, 0:1], x1_of(b)[:, t, :],
                                                    ALU.mult, ALU.add)
                end_.then_inc(res_done, 1)
            for t in range(RT):
                end_ = combine(0, t)
            moments(0, end_)
            normed(eng, x1[:, 0], xn, ln).then_inc(xn_ready, 1)
            xt_lo(0, True)
            turns(eng, turn)

        def pe(eng):
            def x_transposed(b, ks, first=False):
                eng.wait_ge(xn_ready, b + 1)
                for k in ks:
                    if not (first and k < 2):
                        eng.wait_ge(xtl_done, KC * b + k - 1)
                    for t in range(RT):
                        last = eng.transpose(xt_ps[k % 2][:, t * P:(t + 1) * P], xn[:, t, k * P:(k + 1) * P], ident[:])
                    last.then_inc(xt_done, 1)

            def turn(b, first, last):
                def hidden(m):
                    q, g = m % 2, HM * b + m
                    if not (first and m < 2):
                        eng.wait_ge(relu_done, g - 1)
                    for k in range(KC):
                        if m == 0:
                            eng.wait_ge(xtl_done, KC * b + k + 1)
                        for v in (xth, xtl):
                            end_ = eng.matmul(h_ps[q][:], fcT[:, k, m * P:(m + 1) * P], v[:, k, :],
                                              start=(k == 0 and v is xth), stop=(k == KC - 1 and v is xtl))
                    end_.then_inc(hid_done, 1)

                hidden(0)
                for m in range(HM):
                    q = m % 2
                    if m + 1 < HM:
                        hidden(m + 1)
                    if not last and m >= HM - 2:
                        x_transposed(b + 1, (0, 1) if m == HM - 2 else (2, 3))
                    eng.wait_ge(hlo_done, HM * b + m + 1)
                    if m == 0 and not first:
                        eng.wait_ge(res_done, b)
                    for t in range(RT):
                        for h in (hhi, hlo):
                            end_ = eng.matmul(y_ps[:, t, :], h[:, q, t * P:(t + 1) * P], projT[:, m, :],
                                              start=(m == 0 and h is hhi), stop=(m == HM - 1 and h is hlo))
                    end_.then_inc(mlp_used, 1)
            x_transposed(0, range(KC), True)
            turns(eng, turn)

        return dict(sp=sp, pool=pool, act=act, dve=dve, pe=pe)

    WIDTH = [P * (i + 1) for i in range(RT)]
    ORDER = [3, 2, 0, 1]
    BANK_END = [0, 2, 2, 3]
    S_AT = [896, 1024, 512, 0]
    T_WIDTH = [SEQ - P * k for k in range(RT)]
    T_AT = [0, 512, 1024, 896]
    TRI = sum(WIDTH)

    def attention_stage(L, W, V_strip, groups, per_body, per_batch, rotated, xt_d, res_d, dst_d):
        NH = 4 * groups
        HB = 4 * per_body
        bodies = groups // per_body
        batches_per_body = per_body // per_batch if per_body >= per_batch else 1
        VW = P * per_batch
        XB = 1
        n_ = lambda t: f"{t}_{L}"
        st = ExitStack()
        if rotated:
            pth, ptl = (sb(st, n_(t), [P, 2, TRI], F32R) for t in ("pt_hi", "pt_lo"))
        xth = sb(st, n_("axt_hi"), [P, XB, KC, SEQ], F32R)
        xtl = sb(st, n_("axt_lo"), [P, XB, KC, SEQ], F32R)
        if V_strip is None:
            V_strip = strips(st, L)
        stacked = not rotated
        if stacked:
            plain = {w: sb(st, n_(w + "_hi_lo"), [P, 2, SEQ], F32R) for w in "qk"}
            stack = {w: sb(st, n_(w + "_stack"), [3 * HD, 2, HPG, SEQ], F32R) for w in "qk"}
            moved = {w: dram(n_(w + "_moved"), (P, 2, SEQ)) for w in "qk"}
            STACK = dict(q=(0, 0, 1), k=(0, 1, 0))
            moved_out = {w: sem(n_(w + "_moved_out")) for w in "qk"}
            stack_in = {w: sem(n_(w + "_stack_in")) for w in "qk"}
        else:
            qh, ql, kh, kl = (sb(st, n_(t), [P, 2, SEQ], F32R) for t in ("q_hi", "q_lo", "k_hi", "k_lo"))
        vf = sb(st, n_("v"), [P, RT, VW])
        vh, vl = V_strip
        probs = sb(st, n_("p"), [P, 2, TRI])
        if not rotated:
            pth, ptl = (sb(st, n_(t), [P, 2, TRI], F32R) for t in ("pt_hi", "pt_lo"))
        nmax = sb(st, n_("nmax"), [P, 2, RT])
        rsum = sb(st, n_("rsum"), [P, 2, RT, HPG])
        rinv = sb(st, n_("rinv"), [P, RT, HPG])
        oraw = sb(st, n_("o_raw"), [P, SEQ])
        on = sb(st, n_("o_rows"), [P, RT, P])
        oth = sb(st, n_("ot_hi"), [P, per_batch, SEQ], F32R)
        otl = sb(st, n_("ot_lo"), [P, per_batch, SEQ], F32R)
        res = sb(st, n_("res"), [P, 2, D])
        if rotated:
            ra, rb, rot = (sb(st, n_(t), [P, SEQ]) for t in ("ra", "rb", "rot"))
            low = sb(st, "tern_below", [P, HM * D // SLABS], BF16)
            zero = sb(st, "zero", [P, SLOTS])
            table = sb(st, "table", [SC, P])
            zero_done, table_zero, scattered, table_in, tail_zero = (
                sem(n) for n in ("zero_done", "table_zero", "scattered", "table_in", "tail_zero"))
        s_ps = ps(st, n_("s_ps"), [P, 3 * SEQ])
        t_ps = ps(st, n_("t_ps"), [P, 3 * SEQ])
        o_ps = ps(st, n_("o_ps"), [P, SEQ])
        pj = ps(st, n_("pj"), [P, SEQ])
        st.close()
        (s_done, max_done, exp_done, t_done, th_done, tl_done, pv_done, oraw_done, rinv_done, oh_done,
         vh_done, vl_done, pj_done, pj_free, qh_done, ql_done, ro_done) = (sem(n_(t)) for t in (
             "s_done", "max_done", "exp_done", "t_done", "th_done", "tl_done", "pv_done", "oraw_done", "rinv_done",
             "oh_done", "vh_done", "vl_done", "pj_done", "pj_free", "qh_done", "ql_done", "ro_done"))
        strips_zero = sem(n_("strips_zero"))
        xt_in = [sem(n_(f"axt_in{i}")) for i in range(XB)]
        res_in = [sem(n_(f"res_in{i}")) for i in range(2)]
        stored = [sem(n_(f"stored{i}")) for i in range(2)]

        SIGNS_AT = {5: 1, 7: 1, 8: 3, 9: 1, 11: 1, 12: 3, 13: 3, 14: 3, 15: 2, 16: 2}
        def jobs(s):
            out_ = []
            g, left = divmod(s - 6, HPG)
            ended = left == 0 and 0 <= g < groups
            if ended:
                out_ += [("rows", g, 0)]
            for back, parts in ((7, (0, 1)), (8, (2,)), (9, (3,))):
                g, left = divmod(s - back, 4)
                if left == 0 and 0 <= g < groups and (g + 1) % per_batch == 0:
                    out_ += [("out", g, t) for t in parts]
            g, j = s // 4 + 1, s % 4
            if 0 <= g < groups:
                fresh = g % per_batch == 0
                if rotated:
                    out_ += {0: [], 1: [("qA", g, 0), ("qB", g, 0)], 2: [("kA", g, 0), ("kB", g, 0)],
                             3: [("v", g, RT - 1)]}[j]
                else:
                    out_ += {0: [("q", g, 0)], 1: [("k", g, 0)], 2: [("v", g, 0), ("v", g, 1)] if fresh else [],
                             3: [("v", g, 2), ("v", g, 3)] if fresh else []}[j]
            if ended:
                out_ += [("back", (s - 6) // HPG, 0)]
            if rotated:
                before = sum(n for t, n in SIGNS_AT.items() if t < s)
                out_ += [("sign", before + n, 0) for n in range(SIGNS_AT.get(s, 0))]
                if s == NH:
                    out_ += [("table", 0, 0)]
            return out_

        number = {}
        for s in range(-4, NH + 6):
            for job in jobs(s):
                number[job] = len(number)
        uses = sum(len(jobs(s)) for s in range(HB, 2 * HB))

        class At:
            def __init__(self, i=None):
                self.i = i

            def __call__(self, value, per_body_):
                return value if self.i is None else value + per_body_ * (self.i - 1)

            def heads(self, v):
                return self(v, HB)

            def tiles(self, v):
                return self(v, RT * HB)

            def groups(self, v, times=1):
                return self(v, times * per_body)

            def jobs(self, v):
                return self(v, uses)

            def batches(self, v, times=1):
                return self(v, times * batches_per_body)

        def run(eng, step):
            for s in range(-4, HB):
                step(eng, s, At())
            if bodies > 2:
                with eng.Fori(1, bodies - 1) as i:
                    for s in range(HB, 2 * HB):
                        step(eng, s, At(i))
            for s in range(HB * (bodies - 1), NH + 6):
                step(eng, s, At())

        def last_out(g):
            before = ("out", g // per_batch * per_batch - 1, RT - 1)
            return number.get(before)

        def slots_of(s):
            n = len(jobs(s))
            return {0: (), 1: (1,), 2: (0, 1), 3: (0, 1, 3)}.get(n, (0, 1, 2) + (3,) * n)

        def lead(s):
            return sum(slot_ == 0 for slot_ in slots_of(s))

        def pe_jobs(eng, todo, at):
            for job in todo:
                what, g, t = job
                u = number[job]
                b = g // per_batch
                if u:
                    eng.wait_ge(pj_free, at.jobs(u))
                if what in ("q", "qA") and g % per_batch == 0:
                    eng.wait_ge(xt_in[b % XB], at.batches(32 * (b // XB + 1), 32 // XB))
                x_h, x_l = xth[:, b % XB], xtl[:, b % XB]
                if what == "sign":
                    m, n = divmod(g, HM)
                    eng.wait_ge(sign_step, 3 * SLABS * (m + 1))
                    for c in range(KC):
                        last = eng.transpose(pj[:].bitcast(BF16)[:, c * P:(c + 1) * P], sign_block(g, c), ident_b[:])
                    last.then_inc(pj_done, 1)
                    continue
                if what == "table":
                    eng.wait_ge(table_in, 16)
                    eng.transpose(pj[:, 0:SC], table[:], ident[0:SC, 0:SC]).then_inc(pj_done, 1)
                    continue
                if what in ("rows", "back"):
                    if what == "rows":
                        eng.wait_ge(oraw_done, at.groups(g + 1))
                    else:
                        eng.wait_ge(pj_free, at.jobs(number[("rows", g, 0)] + 1))
                    for i in range(RT):
                        src = oraw[:, i * P:(i + 1) * P] if what == "rows" else on[:, i, :]
                        last = eng.transpose(pj[:, i * P:(i + 1) * P], src, ident[:])
                    last.then_inc(pj_done, 1)
                    continue
                if what == "out":
                    eng.wait_ge(pj_free, at.jobs(number[("back", g, 0)] + 1))
                    c = slice(t * P, (t + 1) * P)
                    terms = [(a[:, k, c], w_[:, k, :]) for k in range(per_batch)
                             for a, w_ in ((oth, W["o_hi"]), (oth, W["o_lo"]), (otl, W["o_hi"]))]
                    if rotated:
                        terms += [(W["ones_r"][:, 0:P], W["bo_hi"][:]), (W["ones_r"][:, 0:P], W["bo_lo"][:])]
                    o = pj[:]
                elif what == "v" and rotated:
                    for i in range(RT):
                        c = slice(i * P, (i + 1) * P)
                        terms = [(a[:, k, c], w_[:, k, :]) for k in range(KC)
                                 for a, w_ in ((x_h, W["v_hi"]), (x_h, W["v_lo"]), (x_l, W["v_hi"]))]
                        terms += [(W["ones_r"][:, 0:P], W["bv_hi"][:]), (W["ones_r"][:, 0:P], W["bv_lo"][:])]
                        for n, (a, b_) in enumerate(terms):
                            last = eng.matmul(pj[:, c], a, b_, start=(n == 0), stop=(n == len(terms) - 1))
                    last.then_inc(pj_done, 1)
                    continue
                elif what == "v":
                    c = slice(t * P, (t + 1) * P)
                    terms = [(a[:, k, c], w_[:, k, :]) for k in range(KC)
                             for a, w_ in ((x_h, W["v_hi"]), (x_h, W["v_lo"]), (x_l, W["v_hi"]))]
                    o = pj[:]
                else:
                    w_hi, w_lo = W[what + "_hi"], W[what + "_lo"]
                    c = slice((g % per_batch) * P, (g % per_batch + 1) * P)
                    terms = [(w_[:, k, c], v[:, k, :]) for k in range(KC)
                             for w_, v in ((w_hi, x_h), (w_hi, x_l), (w_lo, x_h))]
                    if rotated:
                        terms += [(W["b" + what + "_hi"][:], W["ones_r"][:]), (W["b" + what + "_lo"][:], W["ones_r"][:])]
                    o = pj[:]
                for n, (a, b_) in enumerate(terms):
                    last = eng.matmul(o, a, b_, start=(n == 0), stop=(n == len(terms) - 1))
                last.then_inc(pj_done, 1)

        def pe_step(eng, s, at):
            if 0 <= s < NH:
                g, j = divmod(s, 4)
                if j == 0:
                    if rotated:
                        eng.wait_ge(ql_done, at.groups(2 * g + 2, 2))
                    else:
                        for w in "qk":
                            eng.wait_ge(stack_in[w], at.groups(48 * (g + 1), 48))
                if s:
                    eng.wait_ge(exp_done, at.tiles(RT * s))
                r = slice(HD * j, HD * (j + 1))
                for i in ORDER:
                    o = s_ps[:, S_AT[i]:S_AT[i] + WIDTH[i]]
                    if stacked:
                        pairs = [(stack["q"][:, g % 2, j], stack["k"][:, g % 2, j])]
                    else:
                        pairs = [(a[r, g % 2], b[r, g % 2]) for a, b in ((qh, kh), (qh, kl), (ql, kh))]
                    for n, (a, b) in enumerate(pairs):
                        eng.matmul(o, a[:, i * P:(i + 1) * P], b[:, 0:WIDTH[i]], start=(n == 0), stop=False)
                    eng.matmul(s_ps[:, S_AT[i] + i * P:S_AT[i] + (i + 1) * P], ident_b[:], mask_b[:],
                               start=False, stop=True).then_inc(s_done, 1)
            todo, slots = jobs(s), slots_of(s)
            put = lambda place: pe_jobs(eng, [job for job, slot_ in zip(todo, slots) if slot_ == place], at)
            put(0)
            m = s - 1
            if 0 <= m < NH:
                eng.wait_ge(exp_done, at.tiles(RT * (m + 1)))
                if m:
                    eng.wait_ge(tl_done, at.heads(m))
                for k in range(RT):
                    for i in range(k, RT):
                        last = eng.transpose(t_ps[:, T_AT[k] + (i - k) * P:T_AT[k] + (i - k + 1) * P],
                                             probs[:, m % 2, S_AT[i] + k * P:S_AT[i] + (k + 1) * P], ident[:])
                last.then_inc(t_done, 1)
            put(1)
            m = s - 2
            if 0 <= m < NH:
                g, j = divmod(m, 4)
                eng.wait_ge(tl_done, at.heads(m + 1))
                if j == 0 and g:
                    eng.wait_ge(oraw_done, at.groups(g))
                if j % 2 == 0:
                    eng.wait_ge(vl_done, at.groups(2 * g + j // 2 + 1, 2))
                for k in range(RT):
                    o = o_ps[:, k * P:SEQ]
                    c = slice(T_AT[k], T_AT[k] + T_WIDTH[k])
                    for n, (a, b) in enumerate(((vh, pth), (vh, ptl), (vl, pth))):
                        last = eng.matmul(o, a[:, k, j * P:(j + 1) * P], b[:, m % 2, c],
                                          start=(j == 0 and k == 0 and n == 0), stop=(j == 3 and k == 3 and n == 2))
                    if k == 0:
                        put(2)
                last.then_inc(pv_done, 1)
            else:
                put(2)
            put(3)

        def strip(t, half):
            return t[:, :, 320 * half:320 * (half + 1)].rearrange("p k (j c) -> p k j c", j=2)[:, :, :, 0:HD]

        def v_of(g, half):
            c = (g % per_batch) * P + 2 * HD * half
            return vf[:, :, c:c + 2 * HD].rearrange("p k (j d) -> p k j d", j=2)

        def strips_due(s):
            if s % 2 == 0 and 0 <= s < NH:
                return s // 4, s % 4 // 2

        def scale_of(what):
            return HD ** -0.5 if what[0] == "q" else 1.0

        def act_jobs(eng, todo, at):
            for job in todo:
                what, g, t = job
                if what == "sign":
                    eng.wait_ge(pj_done, at.jobs(number[job] + 1))
                    nc.scalar.copy(sign_slice(g), pj[:].bitcast(BF16)[:, 0:D].rearrange("p (c q) -> p c q", c=KC)
                                   ).then_inc(pj_free, 1)
                    continue
                if what == "back":
                    eng.wait_ge(pj_done, at.jobs(number[job] + 1))
                    if last_out(g) is not None:
                        eng.wait_ge(pj_done, at.jobs(last_out(g) + 1))
                    nc.scalar.copy(oth[:, g % per_batch, :], pj[:]).then_inc(oh_done, 1)
                    continue
                if what[0] not in "qk" or what.endswith("A"):
                    continue
                if stacked:
                    dst = plain[what][:, 0]
                    if g:
                        eng.wait_ge(moved_out[what], at.groups(16 * g, 16))
                else:
                    dst = (qh if what[0] == "q" else kh)[:, g % 2, :]
                if what.endswith("B"):
                    eng.wait_ge(ro_done, at.groups(2 * g + (what[0] == "k") + 1, 2))
                else:
                    eng.wait_ge(pj_done, at.jobs(number[job] + 1))
                if g >= 2 and not stacked:
                    eng.wait_ge(s_done, at.tiles(RT * 4 * (g - 1)))
                nc.scalar.activation(dst, rot[:] if rotated else pj[:], ACT.Copy,
                                     scale=scale_of(what)).then_inc(qh_done, 1)

        def act_step(eng, s, at):
            if 0 <= s < NH:
                q = s % 2
                g, j = divmod(s, HPG)
                if s >= 2:
                    eng.wait_ge(t_done, at.heads(s - 1))
                if g >= 2 and j == 0:
                    eng.wait_ge(rinv_done, at.groups(g - 1))
                for n, i in enumerate(ORDER):
                    eng.wait_ge(max_done, at.tiles(RT * s + BANK_END[n] + 1))
                    c = slice(S_AT[i], S_AT[i] + WIDTH[i])
                    nc.scalar.activation(probs[:, q, c], s_ps[:, c], ACT.Exp, bias=nmax[:, q, i:i + 1],
                                         accum_out=rsum[:, g % 2, i, j:j + 1]).then_inc(exp_done, 1)
            act_jobs(eng, jobs(s)[:lead(s)], at)
            m = s - 1
            if 0 <= m < NH:
                eng.wait_ge(t_done, at.heads(m + 1))
                if m >= 2:
                    eng.wait_ge(pv_done, at.heads(m - 1))
                nc.scalar.copy(pth[:, m % 2, :], t_ps[:, 0:TRI]).then_inc(th_done, 1)
            if strips_due(s):
                g, half = strips_due(s)
                if half == 0:
                    b = g // per_batch
                    eng.wait_ge(pj_free, at.jobs(number[("v", b * per_batch, RT - 1)] + 1))
                if g:
                    eng.wait_ge(pv_done, at.heads(4 * g - 2 + 2 * half))
                elif half == 0 and not rotated:
                    eng.wait_ge(strips_zero, 2)
                nc.scalar.copy(strip(vh, half), v_of(g, half)).then_inc(vh_done, 1)
            act_jobs(eng, jobs(s)[lead(s):], at)
            if s % HPG == 1 and 0 <= s - 5 < NH:
                g = (s - 5) // HPG
                eng.wait_ge(pv_done, at.heads(HPG * (g + 1)))
                if g:
                    eng.wait_ge(pj_done, at.jobs(number[("rows", g - 1, 0)] + 1))
                nc.scalar.copy(oraw[:], o_ps[:]).then_inc(oraw_done, 1)

        def dve_jobs(eng, todo, at):
            for job in todo:
                what, g, t = job
                u = number[job]
                b = g // per_batch
                if what == "sign":
                    continue
                if what == "table":
                    eng.wait_ge(pj_done, at.jobs(u + 1))
                    eng.tensor_copy(slot_token[:], pj[:, 0:SC]).then_inc(pj_free, 1)
                elif what == "rows":
                    eng.wait_ge(exp_done, at.tiles(RT * HPG * (g + 1)))
                    if g:
                        eng.wait_ge(pj_free, at.jobs(number[("rows", g - 1, 0)] + 1))
                        eng.wait_ge(pj_done, at.jobs(number[("back", g - 1, 0)] + 1))
                    eng.reciprocal(rinv[:], rsum[:, g % 2]).then_inc(rinv_done, 1)
                    eng.wait_ge(rinv_done, at.groups(g + 1))
                    eng.wait_ge(pj_done, at.jobs(u + 1))
                    eng.tensor_tensor(on[:].rearrange("p i (j d) -> p i j d", d=HD),
                                      pj[:].rearrange("p (i j d) -> p i j d", d=HD, j=HPG),
                                      rinv[:].unsqueeze(3).to_broadcast([P, RT, HPG, HD]), ALU.mult).then_inc(pj_free, 1)
                elif what == "back":
                    eng.wait_ge(oh_done, at.groups(g + 1))
                    eng.tensor_tensor(otl[:, g % per_batch, :], pj[:], oth[:, g % per_batch, :].bitcast(F32),
                                      ALU.subtract).then_inc(pj_free, 1)
                elif what == "v":
                    if g and (t == 0 or rotated):
                        eng.wait_ge(vl_done, at.groups(2 * g, 2))
                    eng.wait_ge(pj_done, at.jobs(u + 1))
                    eng.tensor_copy(vf[:].rearrange("p t n -> p (t n)") if rotated else vf[:, t, :], pj[:]).then_inc(pj_free, 1)
                elif what == "out":
                    eng.wait_ge(pj_done, at.jobs(u + 1))
                    eng.wait_ge(res_in[t % 2], at.batches(16 * (2 * b + t // 2 + 1), 32))
                    eng.tensor_tensor(res[:, t % 2, :], pj[:], res[:, t % 2, :], ALU.add).then_inc(pj_free, 1)
                elif what.endswith("A"):
                    eng.wait_ge(pj_done, at.jobs(u + 1))
                    eng.tensor_tensor(ra[:], pj[:], W["cos"][:], ALU.mult).then_inc(pj_free, 1)
                else:
                    turn = 2 * g + (what[0] == "k") + 1
                    src = pj
                    if rotated:
                        eng.wait_ge(pj_done, at.jobs(u + 1))
                        eng.tensor_tensor(rb[:], pj[:], W["sin"][:], ALU.mult).then_inc(pj_free, 1)
                        eng.wait_ge(pj_free, at.jobs(u + 1))
                        eng.tensor_tensor(rot[:], ra[:], rb[:], ALU.add).then_inc(ro_done, 1)
                        src = rot
                        eng.wait_ge(ro_done, at.groups(turn, 2))
                    if stacked:
                        hi, lo = plain[what][:, 0], plain[what][:, 1]
                    else:
                        hi, lo = (t[:, g % 2, :] for t in ((qh, ql) if what[0] == "q" else (kh, kl)))
                    eng.wait_ge(qh_done, at.groups(turn, 2))
                    ins = eng.scalar_tensor_tensor(lo, src[:], scale_of(what), hi.bitcast(F32),
                                                   ALU.mult, ALU.subtract)
                    ins.then_inc(ql_done if rotated else pj_free, 1)

        def dve_step(eng, s, at):
            if 0 <= s < NH:
                q = s % 2
                for n, i in enumerate(ORDER):
                    eng.wait_ge(s_done, at.tiles(RT * s + BANK_END[n] + 1))
                    eng.tensor_reduce(nmax[:, q, i:i + 1], s_ps[:, S_AT[i]:S_AT[i] + WIDTH[i]], AX, ALU.max,
                                      negate=True).then_inc(max_done, 1)
            dve_jobs(eng, jobs(s)[:lead(s)], at)
            m = s - 1
            if 0 <= m < NH:
                eng.wait_ge(th_done, at.heads(m + 1))
                if m >= 2:
                    eng.wait_ge(pv_done, at.heads(m - 1))
                eng.tensor_tensor(ptl[:, m % 2, :], t_ps[:, 0:TRI], pth[:, m % 2, :].bitcast(F32),
                                  ALU.subtract).then_inc(tl_done, 1)
            if strips_due(s):
                g, half = strips_due(s)
                eng.wait_ge(vh_done, at.groups(2 * g + half + 1, 2))
                eng.tensor_tensor(strip(vl, half), v_of(g, half), strip(vh, half).bitcast(F32),
                                  ALU.subtract).then_inc(vl_done, 1)
            dve_jobs(eng, jobs(s)[lead(s):], at)

        res_t = res_d.rearrange("(t p) d -> t p d", p=P)
        dst_t = dst_d.rearrange("(t p) d -> t p d", p=P)

        def load_xt(eng, b, at):
            for t, src in ((xth, xt_d[0]), (xtl, xt_d[1])):
                eng.dma_start(t[:, b % XB].bitcast(F32).rearrange("p k n -> p (k n)"),
                              one(src, at.batches(b), "a p n -> (a p) n")).then_inc(xt_in[b % XB], 16)

        early["xt" + L] = lambda eng: load_xt(eng, 0, At())

        def load_res(eng, b, t, at):
            eng.dma_start(res[:, t % 2, :], one(res_t, at.batches(RT * b + t, RT), "a p d -> (a p) d")
                          ).then_inc(res_in[t % 2], 16)

        batches = groups // per_batch

        def sp_step(eng, s, at):
            if rotated and s == NH:
                eng.wait_ge(pj_done, number[("v", groups - 1, RT - 1)] + 1)
                early["experts"](eng)
            for job in jobs(s):
                what, g, t = job
                b = g // per_batch
                if what == "out":
                    eng.wait_ge(pj_free, at.jobs(number[job] + 1))
                    eng.dma_start(one(dst_t, at.batches(RT * b + t, RT), "a p d -> (a p) d"),
                                  res[:, t % 2, :]).then_inc(stored[t % 2], 16)
                    nb, nt_ = (b, t + 2) if t < 2 else (b + 1, t - 2)
                    if nb < batches:
                        eng.wait_ge(stored[t % 2], at.batches(16 * (2 * b + t // 2 + 1), 32))
                        load_res(eng, nb, nt_, at)
                if stacked and what in ("q", "k"):
                    eng.wait_ge(pj_free, at.jobs(number[job] + 1))
                    settle(eng)
                    if g:
                        eng.wait_ge(stack_in[what], at.groups(48 * g, 48))
                        settle(eng)
                    eng.dma_start(moved[what], plain[what][:].bitcast(F32)).then_inc(moved_out[what], 16)
                    if g >= 2:
                        eng.wait_ge(s_done, at.tiles(RT * HPG * (g - 1)))
                        settle(eng)
                    eng.wait_ge(moved_out[what], at.groups(16 * (g + 1), 16))
                    settle(eng)
                    for n, s_ in enumerate(STACK[what]):
                        eng.dma_start(stack[what][n * HD:(n + 1) * HD, g % 2].bitcast(F32),
                                      moved[what][:, s_, :].rearrange("(j d) n -> d j n", d=HD)
                                      ).then_inc(stack_in[what], 16)
                end_of = ("v", g, RT - 1) if per_batch == 1 else ("k", (b + 1) * per_batch - 1, 0)
                if job == end_of and b + XB < batches:
                    eng.wait_ge(pj_done, at.jobs(number[job] + 1))
                    load_xt(eng, b + XB, at)

        def sp(eng):
            for t in range(2):
                load_res(eng, 0, t, At())
            if rotated:
                times = (TILES - FEWEST) * SLOTS * D // (P * SLOTS)
                eng.wait_ge(zero_done, 1)
                eng.dma_start(y_d[FEWEST * SLOTS:].rearrange("r (h c) -> (r h) c", c=SLOTS).rearrange("(p n) c -> p n c", p=P),
                              zero[:].unsqueeze(1).to_broadcast([P, times, SLOTS])).then_inc(tail_zero, 16)
            run(eng, sp_step)
            if rotated:
                eng.wait_ge(tail_zero, 16)
            for q in range(2):
                eng.wait_ge(stored[q], 16 * 2 * batches)

        def pool(eng):
            if not rotated:
                for t in V_strip:
                    eng.memset(t[:].bitcast(F32), 0.0).then_inc(strips_zero, 1)
                return
            eng.memset(zero[:], 0.0).then_inc(zero_done, 1)
            eng.wait_ge(zero_done, 1)
            eng.dma_start(slot_tok_d.rearrange("(c p) o -> c (p o)", p=P), zero[0:SC, 0:P]).then_inc(table_zero, 16)
            eng.wait_ge(table_zero, 16)
            for k in range(TOPK):
                for t in range(NT):
                    eng.indirect_dma_start(out=slot_tok_d, out_offset=bass.IndirectOffsetOnAxis(
                        ap=slot[:, k, t:t + 1], axis=0), in_=token[:, t:t + 1], in_offset=None).then_inc(scattered, 16)
            ternary_signs(eng, low)
            eng.wait_ge(scattered, 16 * TOPK * NT)
            eng.dma_start(table[:], slot_tok_d.rearrange("(c p) o -> c (p o)", p=P)).then_inc(table_in, 16)
            eng.wait_ge(table_in, 16)

        return dict(sp=sp, pool=pool, act=lambda e: run(e, act_step),
                    dve=lambda e: run(e, dve_step), pe=lambda e: run(e, pe_step))

    def strips(stack, L):
        return [sb(stack, f"v_strip_{s}_{L}", [P, RT, 640], F32R) for s in ("hi", "lo")]

    def with_zero_strips(stage, pair, done):
        def pool(eng):
            for t in pair:
                last = eng.memset(t[:].bitcast(F32), 0.0)
            last.then_inc(done, 1)
            eng.wait_ge(done, 1)
        return dict(stage, pool=pool)

    for s in ("hi", "lo"):
        W0[f"o_{s}"] = sb(layer0, f"w0_o_{s}", [P, 1, D], F32R)
        W0[f"bo_{s}"] = sb(layer0, f"b0_o_{s}", [1, D], F32R)
    W0["ones_r"] = sb(layer0, "ones_r", [1, SEQ], F32R)
    W0["cos"] = sb(layer0, "cos_sb", [P, SEQ])
    W0["sin"] = sb(layer0, "sin_sb", [P, SEQ])
    strip0 = strips(layer0, "l0")
    x_rows = x.rearrange("b t d -> (b t) d")
    out_rows = out.rearrange("b t d -> (b t) d")
    stages = [norm_stage(lambda stack: weights0(W0, strip0, stack)), route_stage(),
              attention_stage("l0", W0, strip0, BATCH, 2, 1, True, xt0_d, x_rows, r0_d)]
    layer0.close()

    stages.append(expert_stage())
    layer1 = ExitStack()
    W1 = {s: sb(layer1, f"w1_{s}", [P, KC, 4 * D], F32R) for s in ("hi", "lo")}
    for n, name in enumerate(("q", "k", "v", "o")):
        for s in ("hi", "lo"):
            W1[f"{name}_{s}"] = W1[s][:, :, n * D:(n + 1) * D]
    stages.append(mlp_stage(W1))
    ternary.close()
    stages.append(attention_stage("l1", W1, None, BATCH * 4, 4, 4, False, xt1_d, r1_d, out_rows))
    layer1.close()

    block = ctx.enter_context(nc.Block())

    def program(eng, name):
        for k, stage in enumerate(stages):
            begin(eng, k)
            stage[name](eng)
            if k + 1 < len(stages):
                end(eng)

    @block.sync
    def _(sp):
        program(sp, "sp")

    @block.gpsimd
    def _(pool):
        program(pool, "pool")

    @block.scalar
    def _(act):
        program(act, "act")

    @block.vector
    def _(dve):
        program(dve, "dve")

    @block.tensor
    def _(pe):
        program(pe, "pe")

    ctx.close()


NAMES = ["L0_attn_x", "L0_attn_Wq", "L0_attn_bq", "L0_attn_Wk", "L0_attn_bk", "L0_attn_Wv", "L0_attn_bv", "L0_attn_Wo",
         "L0_attn_bo", "L0_ffn_w_gate", "L0_ffn_w1", "L0_ffn_w3", "L0_ffn_w2", "L1_attn_w_qkv", "L1_attn_w_out",
         "L1_ffn_w_fc", "L1_ffn_w_proj"]


def kernel(**inputs):
    import numpy as np
    import concourse.bacc as bacc
    from concourse.bass_utils import run_bass_kernel_spmd

    inv_freq = (np.float32(1.0) / np.float32(10000.0) ** (np.arange(HD // 2, dtype=np.float32) * np.float32(2.0) / np.float32(HD))
                ).astype(np.float32)
    angle = (np.arange(SEQ, dtype=np.float32)[None, :] * np.tile(inv_freq, P // (HD // 2))[:, None]).astype(np.float32)

    nc = bacc.Bacc("TRN2", target_bir_lowering=False, num_devices=1)
    arrays, args = {}, []
    for name in NAMES:
        a = np.ascontiguousarray(inputs[name])
        arrays[f"in_{name}"] = a
        args.append(nc.dram_tensor(f"in_{name}", a.shape, mybir.dt.from_np(a.dtype), kind="ExternalInput").ap())
    for name, a in (("cos", np.cos(angle)), ("sin", np.sin(angle))):
        arrays[f"in_{name}"] = a
        args.append(nc.dram_tensor(f"in_{name}", a.shape, F32, kind="ExternalInput").ap())
    args.append(nc.dram_tensor("out_0", (BATCH, SEQ, D), F32, kind="ExternalOutput").ap())
    build(nc, *args)
    r = run_bass_kernel_spmd(nc, [arrays], core_ids=[0])
    return r.results[0]["out_0"]
```
